# Optimizing a Trainium2 kernel written in Bass

```python
import numpy as np
import jax
import jax.numpy as jnp

def _softmax(x, axis=-1):
    return jax.nn.softmax(x, axis=axis)

def _gelu(x):
    return jax.nn.gelu(x, approximate=True)

def _silu(x):
    return jax.nn.silu(x)

def _sigmoid(x):
    return jax.nn.sigmoid(x)

def _layernorm(x, axis=-1, eps=1e-05):
    m = jnp.mean(x, axis=axis, keepdims=True)
    v = jnp.var(x, axis=axis, keepdims=True)
    return (x - m) / jnp.sqrt(v + eps)

def _scatter_add(tgt, idx, src, axis=0):
    return tgt.at[idx].add(src)

def _segment_sum(src, seg, n):
    return jax.ops.segment_sum(src, seg, n)
kernel_name = 'mk_gnn_resnorm_d4_gnn_r8_68a773'

def setup_inputs(seed: int=0):
    np.random.seed(seed)
    _w = jnp.asarray

    def _rec_inputs():
        import jax
        import jax.numpy as jnp
        _gk = jax.random.key(seed)
        x = -0.0003713 + 1 * jax.random.normal(jax.random.fold_in(_gk, 1), (6250, 128), jnp.float32)
        _s = jax.random.randint(jax.random.fold_in(_gk, 2), (50000,), 0, 6250, jnp.int32)
        _d = jax.random.randint(jax.random.fold_in(_gk, 3), (50000,), 0, 6250, jnp.int32)
        _loop = jnp.arange(6250, dtype=jnp.int32)
        src = jnp.concatenate([_s, _d, _loop])
        dst = jnp.concatenate([_d, _s, _loop])
        _o = jnp.argsort(dst, stable=True)
        src = src[_o]
        dst = dst[_o]
        edge_type_8 = jax.random.randint(jax.random.fold_in(_gk, 13), (106250,), 0, 8, jnp.int32)
        edge_weight = jax.random.uniform(jax.random.fold_in(_gk, 14), (106250,), jnp.float32, 0.0, 0.999999)
        return (x, src, dst, edge_type_8, edge_weight)
    x, src, dst, edge_type_8, edge_weight = _rec_inputs()

    def _L0_gnn_setup():
        import jax, jax.numpy as jnp
        import numpy as np
        N_NODES, N_EDGES, D, N_RELS, N_BASES = (12500, 62500, 128, 8, 4)

        def rel_graph_conv(h, src, dst, etype, coef, bases, loopw, bias):
            hs = h[src]
            c = coef[etype]
            m = c[:, 0:1] * (hs @ bases[0])
            for b in range(1, bases.shape[0]):
                m = m + c[:, b:b + 1] * (hs @ bases[b])
            agg = jax.ops.segment_sum(m, dst, num_segments=h.shape[0])
            return agg + h @ loopw + bias
        key = jax.random.key(seed)
        ks = jax.random.split(key, 16)
        s = 1.0 / np.sqrt(D)
        inp = {'feat': jax.random.normal(ks[0], (N_NODES, D), jnp.float32), 'src': jax.random.randint(ks[1], (N_EDGES,), 0, N_NODES, jnp.int32), 'dst': jax.random.randint(ks[2], (N_EDGES,), 0, N_NODES, jnp.int32), 'etype': jax.random.randint(ks[3], (N_EDGES,), 0, N_RELS, jnp.int32)}
        i = 4
        for l in (1, 2, 3):
            inp[f'coef{l}'] = jax.random.normal(ks[i], (N_RELS, N_BASES), jnp.float32)
            i += 1
            inp[f'bases{l}'] = jax.random.normal(ks[i], (N_BASES, D, D), jnp.float32) * s
            i += 1
            inp[f'loopw{l}'] = jax.random.normal(ks[i], (D, D), jnp.float32) * s
            i += 1
            inp[f'bias{l}'] = jnp.zeros((D,), jnp.float32)
        return inp
    _L0_gnn_all = _L0_gnn_setup()
    _L0_gnn_in = {k: v for k, v in _L0_gnn_all.items() if k in ('coef1', 'bases1', 'loopw1', 'bias1', 'coef2', 'bases2', 'loopw2', 'bias2', 'coef3', 'bases3', 'loopw3', 'bias3')}
    del _L0_gnn_all

    def _L1_gnn_setup():
        import jax, jax.numpy as jnp
        import numpy as np
        N_NODES = 6250
        N_EDGES = 78125
        D_IN = 128
        D_OUT = 128
        key = jax.random.key(seed)
        k1, k2, k3, k4, k5, k6 = jax.random.split(key, 6)
        x = jax.random.normal(k1, (N_NODES, D_IN), dtype=jnp.float32)
        row = jax.random.randint(k2, (N_EDGES,), 0, N_NODES, dtype=jnp.int32)
        col = jax.random.randint(k3, (N_EDGES,), 0, N_NODES, dtype=jnp.int32)
        edge_index = jnp.stack([row, col], axis=0)
        edge_weight = jax.random.uniform(k4, (N_EDGES,), dtype=jnp.float32)
        W = jax.random.normal(k5, (D_OUT, 2 * D_IN), dtype=jnp.float32) * (1.0 / np.sqrt(2 * D_IN))
        b = jax.random.normal(k6, (D_OUT,), dtype=jnp.float32) * 0.01
        return {'x': x, 'edge_index': edge_index, 'edge_weight': edge_weight, 'W': W, 'b': b}
    _L1_gnn_all = _L1_gnn_setup()
    _L1_gnn_in = {k: v for k, v in _L1_gnn_all.items() if k in ('W', 'b')}
    del _L1_gnn_all

    def _L2_gnn_setup():
        import jax, jax.numpy as jnp
        import numpy as np
        N_ENT = 12500

        def _rgcn_layer(x, W, SW, b, src, dst, rel):
            xt = jnp.einsum('nd,rde->rne', x, W)
            msg = xt[rel, src]
            agg = jax.ops.segment_sum(msg, dst, num_segments=x.shape[0])
            return jax.nn.relu(agg + x @ SW + b)
        key = jax.random.key(seed)
        ks = jax.random.split(key, 8)
        d, R, E = (128, 8, 75000)
        scale = 1.0 / np.sqrt(d)
        return {'entity_emb': jax.random.normal(ks[0], (N_ENT, d), dtype=jnp.float32), 'w1': jax.random.normal(ks[1], (R, d, d), dtype=jnp.float32) * scale, 'sl1': jax.random.normal(ks[2], (d, d), dtype=jnp.float32) * scale, 'b1': jnp.zeros((d,), dtype=jnp.float32), 'w2': jax.random.normal(ks[3], (R, d, d), dtype=jnp.float32) * scale, 'sl2': jax.random.normal(ks[4], (d, d), dtype=jnp.float32) * scale, 'b2': jnp.zeros((d,), dtype=jnp.float32), 'edge_index': jax.random.randint(ks[5], (2, E), 0, N_ENT, dtype=jnp.int64), 'edge_type': jax.random.randint(ks[6], (E,), 0, R, dtype=jnp.int64)}
    _L2_gnn_all = _L2_gnn_setup()
    _L2_gnn_in = {k: v for k, v in _L2_gnn_all.items() if k in ('w1', 'sl1', 'b1', 'w2', 'sl2', 'b2')}
    del _L2_gnn_all

    def _L3_gnn_setup():
        import jax, jax.numpy as jnp
        import numpy as np
        N_NODES = 6250
        N_EDGES = 80000
        IN_CH = 128
        OUT_CH = 128
        key = jax.random.key(seed)
        k1, k2, k3 = jax.random.split(key, 3)
        x = jax.random.normal(k1, (N_NODES, IN_CH), dtype=jnp.float32)
        edge_index = jax.random.randint(k2, (2, N_EDGES), 0, N_NODES, dtype=jnp.int64)
        W = jax.random.normal(k3, (OUT_CH, 2 * IN_CH), dtype=jnp.float32) * (1.0 / np.sqrt(2 * IN_CH))
        b = jnp.zeros((OUT_CH,), dtype=jnp.float32)
        return {'x': x, 'edge_index': edge_index, 'W': W, 'b': b}
    _L3_gnn_all = _L3_gnn_setup()
    _L3_gnn_in = {k: v for k, v in _L3_gnn_all.items() if k in ('W', 'b')}
    del _L3_gnn_all
    return {'x': x, 'src': src, 'dst': dst, 'edge_type_8': edge_type_8, 'edge_weight': edge_weight, 'L0_gnn_coef1': _L0_gnn_in['coef1'], 'L0_gnn_bases1': _L0_gnn_in['bases1'], 'L0_gnn_loopw1': _L0_gnn_in['loopw1'], 'L0_gnn_bias1': _L0_gnn_in['bias1'], 'L0_gnn_coef2': _L0_gnn_in['coef2'], 'L0_gnn_bases2': _L0_gnn_in['bases2'], 'L0_gnn_loopw2': _L0_gnn_in['loopw2'], 'L0_gnn_bias2': _L0_gnn_in['bias2'], 'L0_gnn_coef3': _L0_gnn_in['coef3'], 'L0_gnn_bases3': _L0_gnn_in['bases3'], 'L0_gnn_loopw3': _L0_gnn_in['loopw3'], 'L0_gnn_bias3': _L0_gnn_in['bias3'], 'L1_gnn_W': _L1_gnn_in['W'], 'L1_gnn_b': _L1_gnn_in['b'], 'L2_gnn_w1': _L2_gnn_in['w1'], 'L2_gnn_sl1': _L2_gnn_in['sl1'], 'L2_gnn_b1': _L2_gnn_in['b1'], 'L2_gnn_w2': _L2_gnn_in['w2'], 'L2_gnn_sl2': _L2_gnn_in['sl2'], 'L2_gnn_b2': _L2_gnn_in['b2'], 'L3_gnn_W': _L3_gnn_in['W'], 'L3_gnn_b': _L3_gnn_in['b']}

def reference(x, src, dst, edge_type_8, edge_weight, L0_gnn_coef1, L0_gnn_bases1, L0_gnn_loopw1, L0_gnn_bias1, L0_gnn_coef2, L0_gnn_bases2, L0_gnn_loopw2, L0_gnn_bias2, L0_gnn_coef3, L0_gnn_bases3, L0_gnn_loopw3, L0_gnn_bias3, L1_gnn_W, L1_gnn_b, L2_gnn_w1, L2_gnn_sl1, L2_gnn_b1, L2_gnn_w2, L2_gnn_sl2, L2_gnn_b2, L3_gnn_W, L3_gnn_b):
    import jax
    import jax.numpy as jnp

    def _L0_gnn_ref(feat, src, dst, etype, coef1, bases1, loopw1, bias1, coef2, bases2, loopw2, bias2, coef3, bases3, loopw3, bias3):
        import jax, jax.numpy as jnp
        import numpy as np
        N_NODES, N_EDGES, D, N_RELS, N_BASES = (12500, 62500, 128, 8, 4)

        def rel_graph_conv(h, src, dst, etype, coef, bases, loopw, bias):
            hs = h[src]
            c = coef[etype]
            m = c[:, 0:1] * (hs @ bases[0])
            for b in range(1, bases.shape[0]):
                m = m + c[:, b:b + 1] * (hs @ bases[b])
            agg = jax.ops.segment_sum(m, dst, num_segments=h.shape[0])
            return agg + h @ loopw + bias
        h = jax.nn.relu(rel_graph_conv(feat, src, dst, etype, coef1, bases1, loopw1, bias1)) + feat
        h_prev = h
        h = jax.nn.relu(rel_graph_conv(h, src, dst, etype, coef2, bases2, loopw2, bias2)) + h_prev
        h_prev = h
        h = jax.nn.relu(rel_graph_conv(h, src, dst, etype, coef3, bases3, loopw3, bias3)) + h_prev
        return h

    def _L1_gnn_ref(x, edge_index, edge_weight, W, b):
        import jax, jax.numpy as jnp
        import numpy as np
        N_NODES = 6250
        N_EDGES = 78125
        D_IN = 128
        D_OUT = 128
        row, col = (edge_index[0], edge_index[1])
        n = x.shape[0]
        msgs = x[col] * edge_weight[:, None]
        agg = jax.ops.segment_sum(msgs, row, num_segments=n)
        deg = jax.ops.segment_sum(edge_weight, row, num_segments=n)
        deg = jnp.clip(deg, 1.0)[:, None]
        h = jnp.concatenate([x, agg / deg], axis=-1)
        return h @ W.T + b

    def _L2_gnn_ref(entity_emb, w1, sl1, b1, w2, sl2, b2, edge_index, edge_type):
        import jax, jax.numpy as jnp
        import numpy as np
        N_ENT = 12500

        def _rgcn_layer(x, W, SW, b, src, dst, rel):
            xt = jnp.einsum('nd,rde->rne', x, W)
            msg = xt[rel, src]
            agg = jax.ops.segment_sum(msg, dst, num_segments=x.shape[0])
            return jax.nn.relu(agg + x @ SW + b)
        src, dst = (edge_index[0], edge_index[1])
        x = _rgcn_layer(entity_emb, w1, sl1, b1, src, dst, edge_type)
        x = _rgcn_layer(x, w2, sl2, b2, src, dst, edge_type)
        return x

    def _L3_gnn_ref(x, edge_index, W, b):
        import jax, jax.numpy as jnp
        import numpy as np
        N_NODES = 6250
        N_EDGES = 80000
        IN_CH = 128
        OUT_CH = 128
        row, col = (edge_index[0], edge_index[1])
        n = x.shape[0]
        agg = jax.ops.segment_sum(x[col], row, num_segments=n)
        deg = jax.ops.segment_sum(jnp.ones((row.shape[0],), dtype=x.dtype), row, num_segments=n)
        deg = jnp.maximum(deg, 1.0)[:, None]
        agg = agg / deg
        out = jnp.concatenate([x, agg], axis=-1)
        return out @ W.T + b
    edge_index = jnp.stack([src, dst])
    x = _layernorm(x + _L0_gnn_ref(x, src, dst, edge_type_8, L0_gnn_coef1, L0_gnn_bases1, L0_gnn_loopw1, L0_gnn_bias1, L0_gnn_coef2, L0_gnn_bases2, L0_gnn_loopw2, L0_gnn_bias2, L0_gnn_coef3, L0_gnn_bases3, L0_gnn_loopw3, L0_gnn_bias3), axis=-1)
    x = _layernorm(x + _L1_gnn_ref(x, edge_index, edge_weight, L1_gnn_W, L1_gnn_b), axis=-1)
    x = _layernorm(x + _L2_gnn_ref(x, L2_gnn_w1, L2_gnn_sl1, L2_gnn_b1, L2_gnn_w2, L2_gnn_sl2, L2_gnn_b2, edge_index, edge_type_8), axis=-1)
    x = _layernorm(x + _L3_gnn_ref(x, edge_index, L3_gnn_W, L3_gnn_b), axis=-1)
    return x

_drawn_inputs = setup_inputs


def setup_inputs(seed=0):
    import zlib

    import numpy as np

    out = dict(_drawn_inputs(seed))
    spreads = {'L0_gnn_bias1': (0.0, 0.49),
     'L0_gnn_bias2': (0.0, 2.0),
     'L0_gnn_bias3': (0.0, 2.0),
     'L2_gnn_b1': (0.0, 0.424),
     'L2_gnn_b2': (0.0, 0.8),
     'L3_gnn_b': (0.0, 0.1)}
    factors = {'L1_gnn_b': 4.822}
    for name, (base, spread) in spreads.items():
        noise = np.random.default_rng([zlib.crc32(name.encode()), seed]).standard_normal(out[name].shape)
        drawn = base * np.exp(spread * noise) if base else spread * noise
        out[name] = jnp.asarray(drawn.astype(out[name].dtype))
    for name, factor in factors.items():
        out[name] = (out[name] * factor).astype(out[name].dtype)
    return out
```

```python
import concourse.bass as bass
from concourse import mybir
from contextlib import ExitStack


F32 = mybir.dt.float32
I32 = mybir.dt.int32
ALU = mybir.AluOpType
ACT = mybir.ActivationFunctionType
AX = mybir.AxisListType
DVE = mybir.EngineType.DVE
SP = mybir.EngineType.SP

D = 128
N_NODES = 6250
N_EDGES = 106250
N_RELS = 8
N_BASES = 4
WIN = 16
KEYS = WIN * N_RELS
HALF = 8
RING = 2 * HALF
BLOCKS = 8
BLOCK = 104
TILES = BLOCKS * BLOCK
TURNS = TILES // RING
CHUNK = 512
SUB = CHUNK // D
CHUNKS = -(-N_NODES // CHUNK)
PAIRS = CHUNKS // 2
NP = CHUNKS * CHUNK
LAST = N_NODES - (CHUNKS - 1) * CHUNK
MAX_PASSES = -(-N_NODES // WIN)
assert sum((27, 26)) * D == NP + D
FAR = 100000.0
EPS = 1e-5
SHARES = 4
SHARE_ROWS = NP + D
COLS = D + 1
ZERO_ROWS = (27, 26)

REL, MEAN = "relational", "mean"
LAYERS = [
    dict(kind=REL, src="x", lin=0, add=("x",), norm=False),
    dict(kind=REL, src="h", lin=1, add=("h",), norm=False),
    dict(kind=REL, src="h", lin=2, add=("h", "x"), norm=True),
    dict(kind=MEAN, mean=0, weighted=True, norm=True, bias=5),
    dict(kind=REL, src="x", lin=3, add=(), norm=False),
    dict(kind=REL, src="h", lin=4, add=("x",), norm=True),
    dict(kind=MEAN, mean=1, weighted=False, norm=True, bias=6),
]
REL_BEFORE = [sum(x["kind"] == REL for x in LAYERS[:n]) for n in range(len(LAYERS) + 1)]
MEAN_BEFORE = [sum(x["kind"] == MEAN for x in LAYERS[:n]) for n in range(len(LAYERS) + 1)]
NORM_BEFORE = [sum(x["norm"] for x in LAYERS[:n]) for n in range(len(LAYERS) + 1)]
KEPT_BEFORE = [sum(not x["norm"] for x in LAYERS[:n]) for n in range(len(LAYERS) + 1)]


def chunk_pairs(eng, step):
    with eng.Fori(0, PAIRS) as i:
        step([(i * 2, 0, i), (i * 2 + 1, 1, i)])
    step([(CHUNKS - 1, 0, PAIRS)])


def cols(c):
    return bass.ds(c * CHUNK, CHUNK)


def build(nc, x, src, dst, etype, eweight, coefs, bases, loops, rel_ws, mean_ws, biases, out):
    with ExitStack() as ctx:
        def sb(name, shape, dt=F32):
            return ctx.enter_context(nc.sbuf_tensor(name, shape, dt))

        def bank(name):
            return ctx.enter_context(nc.psum_tensor(name, [128, 512], F32))

        def sem(name):
            return ctx.enter_context(nc.semaphore(name))

        table = nc.dram_tensor("h_table", (NP, D), F32, kind="Internal").ap()
        src_pad = nc.dram_tensor("src_pad", (TILES * D,), I32, kind="Internal").ap()
        shares = [[nc.dram_tensor(f"share{m}_{a}", (SHARE_ROWS, COLS), F32, kind="Internal").ap()
                   for a in range(SHARES)] for m in range(2)]

        xT = sb("xT", [D, NP])
        hT = sb("hT", [D, NP])
        acc = sb("acc", [D, NP])
        nodes = {"x": xT, "h": hT}
        edges_i = sb("edges_i", [D, 3, BLOCKS * D], I32)
        src_i, dst_i, type_i = (edges_i[0:BLOCK, n, :].rearrange("p (c e) -> p c e", e=D) for n in range(3))
        low = sb("low", [BLOCK, BLOCKS])
        high = sb("high", [BLOCK, BLOCKS])
        span = sb("span", [BLOCK, 1])
        srcT = sb("srcT", [D, TILES + RING])
        offT = sb("offT", [D, TILES])
        keyT = sb("keyT", [D, TILES])
        wgtT = sb("wgtT", [D, TILES])
        to_spareT = sb("to_spareT", [D, TILES])
        first_window = sb("first_window", [1, TILES], I32)
        window = sb("window", [1, TILES], I32)
        passes = sb("passes", [1, 1], I32)
        span_row = sb("span_row", [1, 2])
        span_i = sb("span_i", [1, 1], I32)
        ident = sb("ident", [128, 128])
        ones = sb("ones", [128, 128])
        iota = sb("iota", [128, KEYS + WIN])
        eps = sb("eps", [128, 1])
        lane = sb("lane", [128, 1])
        lane_i = sb("lane_i", [128, 1], I32)
        before = sb("before", [128, 128])
        basis = sb("basis", [D, 3, N_BASES, D])
        rel_w = sb("rel_w", [D, 2, N_RELS, D])
        mix_w = sb("mix_w", [D, N_RELS, D])
        loop_w = sb("loop_w", [D, 5, D])
        mean_w = sb("mean_w", [D, 2, 2 * D])
        mean_wT = sb("mean_wT", [D, 2, 2, D])
        bias = sb("bias", [D, 7])
        coef_row = sb("coef_row", [1, 3 * N_RELS * N_BASES])
        coef = sb("coef", [128, 3, N_RELS, N_BASES])
        idx = sb("idx", [D, 2, HALF], I32)
        rows_in = sb("rows_in", [D, RING, D])
        onehot = sb("onehot", [D, RING, KEYS])
        sums = sb("sums", [D, 2, N_RELS, HALF, WIN])
        loaded = [t.rearrange("p (c e) -> p c e", e=D) for t in (
            onehot[0:BLOCK, 0:HALF, :].rearrange("p s k -> p (s k)"),
            onehot[0:BLOCK, HALF:RING, :].rearrange("p s k -> p (s k)"),
            sums[0:BLOCK, 0, :, :, :].rearrange("p r t v -> p (r t v)"),
            sums[0:BLOCK, 1, :, :, :].rearrange("p r t v -> p (r t v)"))]
        src_f, dst_f, type_f, wgt = loaded
        src_all = edges_i[:, 0:2, :]
        near = sb("near", [D, RING, WIN])
        same = onehot
        repeats = sb("repeats", [D, 2, HALF])
        place_f = sb("place_f", [D, 2, HALF])
        place = sb("place", [D, 2, HALF], I32)
        win_rows = rows_in[0:WIN, :, :]
        spread = sums[0:WIN, :, :, :, :].rearrange("p h r t v -> p (h r t v)")
        scat = sb("scat", [D, RING, COLS])
        shares_in = sb("shares_in", [D, 2, SHARES, SUB, COLS])
        deg = sb("deg", [D, 2, SUB])
        diag = sb("diag", [D, 2, SUB, D])
        y = sb("y", [D, 2, CHUNK])
        mean = sb("mean", [D, 2, CHUNK])
        unused = mean[:, :, :].rearrange("p b n -> p (b n)").rearrange("p (s d) -> p s d", d=D)
        rows = sb("rows", [D, 2, SUB, D])
        stats = sb("stats", [128, 2, SUB, 6])
        mv = sb("mv", [128, 2, SUB, 2])
        std = sb("std", [128, 2, SUB])
        rstd = sb("rstd", [128, 2, SUB])

        SUM = [bank("sum0"), bank("sum1")]
        MSG = [bank("msg0"), bank("msg1")]
        LIN = [bank("lin0"), bank("lin1")]
        IOTA = bank("iota_ps")

        consts_set = sem("consts_set")
        cleared = sem("cleared")
        src_in, dst_in, type_in, wgt_in = sem("src_in"), sem("dst_in"), sem("type_in"), sem("wgt_in")
        weights_in = sem("weights_in")
        dve_step = sem("dve_step")
        src_cast, off_set, key_set, low_set = sem("src_cast"), sem("off_set"), sem("key_set"), sem("low_set")
        turned_in = sem("turned_in")
        tables_set = sem("tables_set")
        wrapped = sem("wrapped")
        row_read = sem("row_read")
        passes_set = sem("passes_set")
        idx_ready = [sem(f"idx_ready{h}") for h in range(2)]
        gathered = [sem(f"gathered{q}") for q in range(4)]
        onehot_ready = [sem(f"onehot_ready{q}") for q in range(4)]
        summed = [sem(f"summed{q}") for q in range(4)]
        evacuated = [sem(f"evacuated{q}") for q in range(4)]
        messaged = [sem(f"messaged{h}") for h in range(2)]
        added = sem("added")
        pass_moved = sem("pass_moved")
        comparands_moved = sem("comparands_moved")
        waits_passed = sem("waits_passed")
        src_padded = sem("src_padded")
        window_set = sem("window_set")
        win_in = [sem(f"win_in{q}") for q in range(4)]
        src_all_in = [sem(f"src_all_in{h}") for h in range(2)]
        select_ready = [sem(f"select_ready{q}") for q in range(4)]
        place_ready = [sem(f"place_ready{h}") for h in range(2)]
        place_step = sem("place_step")
        spread_ready = [sem(f"spread_ready{q}") for q in range(4)]
        spread_out = [sem(f"spread_out{q}") for q in range(4)]
        expanded = [sem(f"expanded{q}") for q in range(4)]
        scat_ready = [sem(f"scat_ready{q}") for q in range(4)]
        scattered = [sem(f"scattered{a}") for a in range(SHARES)]
        quads_left = sem("quads_left")
        shares_clear = sem("shares_clear")
        shares_landed = [sem(f"shares_landed{b}") for b in range(2)]
        diag_ready, agg_turned = sem("diag_ready"), sem("agg_turned")
        acc_lin, acc_set = sem("acc_lin"), sem("acc_set")
        deg_step, mean_ready, lin_done = sem("deg_step"), sem("mean_ready"), sem("lin_done")
        part = sem("part")
        y_ready, y_kept, turned = sem("y_ready"), sem("y_kept"), sem("turned")
        stats_done, var_ready, std_ready, rstd_done = sem("stats_done"), sem("var_ready"), sem("std_ready"), sem("rstd_done")
        rows_ready = sem("rows_ready")
        rows_dma = [sem(f"rows_dma{b}") for b in range(2)]
        back_turned, x_kept = sem("back_turned"), sem("x_kept")

        block = ctx.enter_context(nc.Block())

        FULL = BLOCKS - 1
        TAIL = N_EDGES - FULL * BLOCK * D
        TAIL_ROWS, TAIL_LAST = TAIL // D, TAIL % D
        def dma_before(l, b):
            return (l + 1) * (CHUNKS - PAIRS if b == 0 else PAIRS)

        def dma_stages(l):
            return dma_before(l, 0), dma_before(l, 1)

        CLEARS = 16 * 2 * SHARES * len(ZERO_ROWS)
        OPENED = 16
        zeros = hT[:, 0:max(ZERO_ROWS) * COLS]

        def shares_before(m, b):
            return m * (CHUNKS - PAIRS if b == 0 else PAIRS)

        def count(P, p, layers_before, i):
            return P * (layers_before * TURNS) + p * TURNS + i

        def apart(eng):
            eng.sem_inc(waits_passed, 1)

        @block.sync
        def _(sp):
            sp.wait_ge(cleared, 4)
            for view, tile, landed in ((src, src_i, src_in), (dst, dst_i, dst_in),
                                       (etype, type_i, type_in), (eweight, wgt, wgt_in)):
                body = FULL * BLOCK * D
                sp.dma_start(tile[:, 0:FULL, :],
                             view[0:body].rearrange("(c p e) -> p c e", p=BLOCK, e=D)).then_inc(landed, 16)
                sp.dma_start(tile[0:TAIL_ROWS, FULL, :],
                             view[body:body + TAIL_ROWS * D].rearrange("(p e) -> p e", e=D)).then_inc(landed, 16)
                sp.dma_start(tile[TAIL_ROWS:TAIL_ROWS + 1, FULL, 0:TAIL_LAST],
                             view[body + TAIL_ROWS * D:N_EDGES].rearrange("(p e) -> p e", p=1)).then_inc(landed, 16)
            sp.wait_ge(src_in, 48)
            sp.dma_start(src_pad.rearrange("(c p e) -> p c e", p=BLOCK, e=D), src_i).then_inc(src_padded, 16)
            for c in range(CHUNKS):
                sp.wait_ge(back_turned, c + 1)
                if c < CHUNKS - 1:
                    sp.dma_start(rows[:, c % 2, :, :],
                                 x[c * CHUNK:(c + 1) * CHUNK, :].rearrange("(k p) d -> p k d", p=D))\
                      .then_inc(rows_dma[c % 2], 16)
                else:
                    sp.dma_start(rows[0:LAST, c % 2, 0, :], x[c * CHUNK:N_NODES, :]).then_inc(rows_dma[c % 2], 16)
            sp.wait_ge(cleared, 5)
            for m in range(2):
                for a in range(SHARES):
                    view = shares[m][a].rearrange("(p r) c -> p r c", p=D)
                    for n, at in zip(ZERO_ROWS, (0, ZERO_ROWS[0])):
                        sp.dma_start(view[:, at:at + n, :],
                                     zeros[:, 0:n * COLS].rearrange("p (r c) -> p r c", c=COLS)).then_inc(shares_clear, 16)
            sp.wait_ge(src_padded, 16)
            sp.wait_ge(passes_set, 1)
            P = sp.value_load(passes[0:1, 0:1], min_val=1, max_val=MAX_PASSES)
            for l, layer in enumerate(LAYERS):
                m = MEAN_BEFORE[l]
                if layer["kind"] == MEAN:
                    for b in range(2):
                        sp.wait_ge(rows_dma[b], 16 * dma_before(l, b))
                    with sp.Fori(0, P) as p:
                        sp.wait_ge(window_set, P * m + p + (m + 1))
                        apart(sp)
                        with sp.Fori(0, TURNS) as i:
                            k = sp.snap(count(P, p, m, i))
                            for h in range(2):
                                _, starts = nc.values_load_multi_w_load_instructions(
                                    window[0:1, bass.ds(i * RING + HALF * h, HALF)], engines=[SP], min_val=0,
                                    max_val=NP - WIN,
                                    skip_runtime_bounds_check_because="starts are destinations, held to NP - WIN on the chip")
                                sp.wait_ge(select_ready[2 * h + 1], k + 1)
                                half = src_pad[bass.ds(i * (RING * D) + HALF * h * D, HALF * D)]
                                sp.dma_start(src_all[:, h, :], half.partition_broadcast(D)).then_inc(src_all_in[h], 16)
                                for s in range(HALF):
                                    q = 2 * h + s // 4
                                    if s % 4 == 0:
                                        sp.wait_ge(expanded[q], k + 1)
                                    sp.dma_start(win_rows[:, HALF * h + s, :],
                                                 table[bass.ds(starts[s], WIN), :]).then_inc(win_in[q], 16)
                    for a in range(SHARES):
                        sp.wait_ge(scattered[a], P * (64 * TURNS * (m + 1)) + OPENED)

                def load_shares(c, b):
                    sp.wait_ge(agg_turned, c + m * CHUNKS + 1)
                    for a in range(SHARES):
                        sp.dma_start(shares_in[:, b, a, :, :],
                                     shares[m][a][cols(c), :].rearrange("(k p) d -> p k d", p=D)).then_inc(shares_landed[b], 16)

                def store(c, b):
                    sp.wait_ge(rows_ready, c + l * CHUNKS + 3)
                    if l < len(LAYERS) - 1:
                        sp.dma_start(table[cols(c), :].rearrange("(k p) d -> p k d", p=D),
                                     rows[:, b, :, :]).then_inc(rows_dma[b], 16)
                    elif type(c) is int and c == CHUNKS - 1:
                        sp.dma_start(out[c * CHUNK:N_NODES, :], rows[0:LAST, b, 0, :]).then_inc(rows_dma[b], 16)
                    else:
                        sp.dma_start(out[cols(c), :].rearrange("(k p) d -> p k d", p=D),
                                     rows[:, b, :, :]).then_inc(rows_dma[b], 16)

                if layer["kind"] == REL:
                    def stores(steps):
                        for c, b, i in steps:
                            store(c, b)
                    chunk_pairs(sp, stores)
                else:
                    load_shares(0, 0)
                    load_shares(1, 1)
                    with sp.Fori(0, PAIRS - 1) as i:
                        for b in range(2):
                            load_shares(i * 2 + 2 + b, b)
                        for b in range(2):
                            store(i * 2 + b, b)
                    load_shares(CHUNKS - 1, 0)
                    for c in range(CHUNKS - 3, CHUNKS):
                        store(c, c % 2)
            for b in range(2):
                sp.wait_ge(rows_dma[b], 16 * dma_before(len(LAYERS), b))

        @block.gpsimd
        def _(pool):
            for tile, value in ((src_i, 0), (dst_i, int(FAR)), (type_i, 0), (wgt, 0.0)):
                nc.gpsimd.memset(tile[:, FULL, :], value).then_inc(cleared, 1)
            nc.gpsimd.memset(ident[:, :], 0.0).then_inc(consts_set, 1)
            nc.gpsimd.memset(ones[:, :], 1.0).then_inc(consts_set, 1)
            nc.gpsimd.memset(eps[:, :], EPS).then_inc(consts_set, 1)
            nc.gpsimd.iota(iota[:, 0:KEYS].rearrange("p (r v) -> p r v", v=WIN), [[1, N_RELS], [N_RELS, WIN]],
                           base=0, channel_multiplier=0, allow_small_or_imprecise_dtypes=True).then_inc(consts_set, 1)
            nc.gpsimd.iota(iota[:, KEYS:KEYS + WIN], [[1, WIN]], base=0, channel_multiplier=0,
                           allow_small_or_imprecise_dtypes=True).then_inc(consts_set, 1)
            pool.wait_ge(consts_set, 5)
            nc.gpsimd.affine_select(out=ident[:, :], in_=ident[:, :], compare_op=ALU.not_equal, fill=1.0, base=0,
                                    pattern=[[-1, 128]], channel_multiplier=1).then_inc(consts_set, 1)
            nc.gpsimd.iota(lane[:, :], [[0, 1]], base=NP, channel_multiplier=1,
                           allow_small_or_imprecise_dtypes=True).then_inc(consts_set, 1)
            nc.gpsimd.iota(lane_i[:, :], [[0, 1]], base=NP, channel_multiplier=1).then_inc(consts_set, 1)
            nc.gpsimd.affine_select(out=before[:, :], in_=ones[:, :], compare_op=ALU.is_gt, fill=0.0, base=0,
                                    pattern=[[-1, 128]], channel_multiplier=1).then_inc(consts_set, 1)
            nc.gpsimd.memset(zeros, 0.0).then_inc(cleared, 1)
            pool.sem_inc(quads_left, 3)
            pool.wait_ge(passes_set, 1)
            P = pool.value_load(passes[0:1, 0:1], min_val=1, max_val=MAX_PASSES)
            for l, layer in enumerate(LAYERS):
                if layer["kind"] == MEAN:
                    m = MEAN_BEFORE[l]
                    if m == 0:
                        pool.wait_ge(shares_clear, CLEARS)
                        pool.wait_ge(x_kept, 2 + CHUNKS * (1 + NORM_BEFORE[l]))
                        for a in range(SHARES):
                            nc.gpsimd.indirect_dma_start(
                                out=shares[m][a], out_offset=bass.IndirectOffsetOnAxis(ap=lane_i[:, 0:1], axis=0),
                                in_=xT[:, 0:COLS], in_offset=None, compute_op=ALU.add).then_inc(scattered[a], 16)
                    with pool.Fori(0, P) as p:
                        with pool.Fori(0, TURNS) as i:
                            k = pool.snap(count(P, p, m, i))
                            for q in range(4):
                                for a in range(SHARES):
                                    if a == 0:
                                        pool.wait_ge(scat_ready[q], k + 2)
                                    pool.wait_ge(scattered[a], k * 64 + (OPENED + 16 * q))
                                    if a < SHARES - 1:
                                        apart(pool)
                                    else:
                                        pool.sem_inc(quads_left, 1)
                                    nc.gpsimd.indirect_dma_start(
                                        out=shares[m][a], out_offset=bass.IndirectOffsetOnAxis(
                                            ap=place[:, q // 2, 4 * (q % 2) + a:4 * (q % 2) + a + 1], axis=0),
                                        in_=scat[:, 4 * q + a, :], in_offset=None, compute_op=ALU.add,
                                    ).then_inc(scattered[a], 16)
                    continue
                r = REL_BEFORE[l]
                rows_of = x if l == 0 else table
                if l:
                    for b in range(2):
                        pool.wait_ge(rows_dma[b], 16 * dma_before(l, b))
                with pool.Fori(0, P) as p:
                    with pool.Fori(0, TURNS) as i:
                        k = pool.snap(count(P, p, r, i))
                        for h in range(2):
                            pool.wait_ge(idx_ready[h], k + 1)
                            pool.wait_ge(summed[2 * h + 1], k + 1)
                            apart(pool)
                            for s in range(HALF):
                                nc.gpsimd.indirect_dma_start(
                                    out=rows_in[:, HALF * h + s, :], out_offset=None, in_=rows_of[:, :],
                                    in_offset=bass.IndirectOffsetOnAxis(ap=idx[:, h, s:s + 1], axis=0),
                                ).then_inc(gathered[2 * h + s // 4], 16)

        @block.scalar
        def _(act):
            act.sem_inc(evacuated[2], 1)
            act.sem_inc(evacuated[3], 1)
            for q in range(4):
                act.sem_inc(scat_ready[q], 1)
            act.sem_inc(spread_out[2], 1)
            act.sem_inc(spread_out[3], 1)
            act.sem_inc(acc_set, 2)
            act.sem_inc(y_kept, 2)
            act.sem_inc(x_kept, 2)
            loads = 0
            for n in range(3):
                act.dma_start(coef_row[:, n * N_RELS * N_BASES:(n + 1) * N_RELS * N_BASES],
                              coefs[n].rearrange("(o r) b -> o (r b)", o=1)).then_inc(weights_in, 16)
                act.dma_start(basis[:, n, :, :], bases[n].rearrange("b i o -> i b o")).then_inc(weights_in, 16)
                loads += 2
            for n in range(2):
                act.dma_start(rel_w[:, n, :, :], rel_ws[n].rearrange("r i o -> i r o")).then_inc(weights_in, 16)
                act.dma_start(mean_w[:, n, :], mean_ws[n]).then_inc(weights_in, 16)
                loads += 2
            for n in range(5):
                act.dma_start(loop_w[:, n, :], loops[n]).then_inc(weights_in, 16)
                loads += 1
            for n in range(7):
                act.dma_start(bias[:, n:n + 1], biases[n].rearrange("(p o) -> p o", o=1)).then_inc(weights_in, 16)
                loads += 1
            copied = 0
            for n, (tile, banks) in enumerate(((srcT, SUM), (keyT, MSG), (offT, LIN), (wgtT, SUM))):
                for b in range(2):
                    act.wait_ge(turned_in, 2 * n + b + 1)
                    act.activation(tile[:, b * 4 * BLOCK:(b + 1) * 4 * BLOCK], banks[b][:, 0:4 * BLOCK],
                                   ACT.Copy).then_inc(tables_set, 1)
                    copied += 1
                if n == 0:
                    act.wait_ge(tables_set, 2)
                    act.activation(srcT[:, TILES:TILES + RING], srcT[:, 0:RING], ACT.Copy).then_inc(wrapped, 1)
                    for h in range(2):
                        act.activation(idx[:, h, :], srcT[:, HALF * h:HALF * (h + 1)], ACT.Copy).then_inc(idx_ready[h], 1)
                    act.wait_ge(wrapped, 1)
            act.wait_ge(turned_in, 11)
            act.activation(mean_wT[:, :, :, :].rearrange("p n s o -> p (n s o)"), MSG[0][:, :], ACT.Copy).then_inc(tables_set, 1)
            act.wait_ge(turned_in, 12)
            act.activation(coef[:, :, :, :].rearrange("p n r b -> p (n r b)"), MSG[1][:, 0:3 * N_RELS * N_BASES],
                           ACT.Copy).then_inc(tables_set, 1)
            act.wait_ge(weights_in, 16 * loads)

            def keep_x(stage):
                def step(steps):
                    for c, b, i in steps:
                        act.wait_ge(back_turned, c + stage * CHUNKS + 3)
                        act.activation(xT[:, cols(c)], MSG[b][:, :], ACT.Copy).then_inc(x_kept, 1)
                return step

            chunk_pairs(act, keep_x(0))
            act.wait_ge(passes_set, 1)
            P = act.value_load(passes[0:1, 0:1], min_val=1, max_val=MAX_PASSES)
            for l, layer in enumerate(LAYERS):
                rel = layer["kind"] == REL
                r = REL_BEFORE[l]
                if rel:
                    def start_acc(steps):
                        for c, b, i in steps:
                            act.wait_ge(acc_lin, c + r * CHUNKS + 1)
                            act.activation(acc[:, cols(c)], LIN[b][:, :], ACT.Identity,
                                           bias=bias[:, layer["lin"]:layer["lin"] + 1]).then_inc(acc_set, 1)
                    chunk_pairs(act, start_acc)
                    with act.Fori(0, P) as p:
                        with act.Fori(0, TURNS) as i:
                            k = act.snap(count(P, p, r, i))
                            for h in range(2):
                                act.wait_ge(messaged[h], k + 1)
                                for q in (2 * h, 2 * h + 1):
                                    act.wait_ge(summed[q], k + 1 + q % 2)
                                    act.activation(
                                        sums[:, h, :, 4 * (q % 2):4 * (q % 2) + 4, :].rearrange("p r t v -> p t r v"),
                                        SUM[q % 2][:, :].rearrange("p (t r v) -> p t r v", t=4, v=WIN),
                                        ACT.Copy).then_inc(evacuated[q], 1)
                                act.activation(idx[:, h, :], srcT[:, bass.ds((i + 1) * RING + h * HALF, HALF)],
                                               ACT.Copy).then_inc(idx_ready[h], 1)
                else:
                    m = MEAN_BEFORE[l]
                    with act.Fori(0, P) as p:
                        with act.Fori(0, TURNS) as i:
                            k = act.snap(count(P, p, m, i))
                            for h in range(2):
                                quads = (2 * h, 2 * h + 1)
                                for q in quads:
                                    act.wait_ge(spread_ready[q], k + 1 + q % 2)
                                    act.wait_ge(expanded[q], k + 1)
                                    act.activation(spread[:, q * 512:(q + 1) * 512], SUM[q % 2][0:WIN, :],
                                                   ACT.Copy).then_inc(spread_out[q], 1)
                                for q in quads:
                                    four = slice(4 * (q % 2), 4 * (q % 2) + 4)
                                    act.wait_ge(place_ready[h], k + 1)
                                    act.wait_ge(quads_left, k * 4 + (q + 1))
                                    act.activation(place[:, h, four], place_f[:, h, four], ACT.Copy)
                                    act.wait_ge(expanded[q], k + 2)
                                    act.activation(scat[:, 4 * q:4 * q + 4, 0:D],
                                                   MSG[q % 2][:, :].rearrange("p (t d) -> p t d", d=D), ACT.Copy)
                                    act.activation(scat[:, 4 * q:4 * q + 4, D], LIN[q % 2][:, 0:4],
                                                   ACT.Copy).then_inc(scat_ready[q], 1)
                if not layer["norm"]:
                    def keep(steps):
                        for c, b, i in steps:
                            act.wait_ge(y_ready, c + l * CHUNKS + 1)
                            act.activation(hT[:, cols(c)], y[:, b, :], ACT.Copy).then_inc(y_kept, 1)
                            act.wait_ge(turned, c + l * CHUNKS + 3)
                            act.wait_ge(rows_dma[b], i * 16 + 16 * dma_stages(l)[b])
                            act.activation(rows[:, b, :, :].rearrange("p k d -> p (k d)"), SUM[b][:, :],
                                           ACT.Copy).then_inc(rows_ready, 1)
                    if l == 0:
                        act.wait_ge(shares_clear, CLEARS)
                    chunk_pairs(act, keep)
                else:
                    n = NORM_BEFORE[l]

                    def deviate(steps):
                        if not rel:
                            for c, b, i in steps:
                                act.wait_ge(agg_turned, c + m * CHUNKS + 3)
                                act.activation(mean[:, b, :], SUM[b][:, :], ACT.Copy).then_inc(mean_ready, 1)
                        for c, b, i in steps:
                            act.wait_ge(var_ready, c + n * CHUNKS + 1)
                            act.activation(std[:, b, :], mv[:, b, :, 1], ACT.Sqrt, bias=eps[:, 0:1]).then_inc(std_ready, 1)
                        if l < len(LAYERS) - 1:
                            keep_x(n + 1)(steps)
                    chunk_pairs(act, deviate)

        @block.tensor
        def _(pe):
            for q in (1, 3):
                pe.sem_inc(summed[q], 1)
            for h in range(2):
                pe.sem_inc(messaged[h], 1)
            for q in (1, 3):
                pe.sem_inc(spread_ready[q], 1)
            for q in range(4):
                pe.sem_inc(expanded[q], 1)
            pe.sem_inc(agg_turned, 2)
            pe.sem_inc(turned, 2)
            pe.sem_inc(back_turned, 2)
            pe.wait_ge(consts_set, 6)

            def turn_table(tile, banks):
                for b in range(2):
                    for c in range(4):
                        last = nc.tensor.transpose(banks[b][:, c * BLOCK:(c + 1) * BLOCK], tile[:, 4 * b + c, :],
                                                   ident[0:BLOCK, 0:BLOCK])
                    last.then_inc(turned_in, 1)

            pe.wait_ge(src_cast, 1)
            turn_table(src_f, SUM)
            pe.wait_ge(key_set, 1)
            turn_table(type_f, MSG)
            turn_table(dst_f, LIN)
            pe.wait_ge(wgt_in, 48)
            pe.wait_ge(tables_set, 2)
            turn_table(wgt, SUM)
            pe.wait_ge(tables_set, 4)
            for b in range(2):
                for c in range(4):
                    last = nc.tensor.matmul(MSG[b][0:1, c * BLOCK:(c + 1) * BLOCK], low[:, 4 * b + c:4 * b + c + 1],
                                            ident[0:BLOCK, 0:BLOCK], start=True, stop=True)
            pe.wait_ge(tables_set, 6)
            nc.tensor.matmul(LIN[0][0:1, 0:BLOCK], span[:, :], ident[0:BLOCK, 0:BLOCK],
                             start=True, stop=True).then_inc(turned_in, 2)
            pe.wait_ge(row_read, 1)
            pe.wait_ge(weights_in, 16 * 22)
            for n in range(2):
                for s in range(2):
                    last = nc.tensor.transpose(MSG[0][:, (2 * n + s) * D:(2 * n + s + 1) * D],
                                               mean_w[:, n, s * D:(s + 1) * D], ident[:, :])
            last.then_inc(turned_in, 1)
            nc.tensor.matmul(MSG[1][:, 0:3 * N_RELS * N_BASES], ones[0:1, :], coef_row[:, :],
                             start=True, stop=True).then_inc(turned_in, 1)
            pe.wait_ge(tables_set, 10)

            def back(stage, c, b):
                pe.wait_ge(x_kept, c + stage * CHUNKS + 1)
                for s in range(SUB):
                    last = nc.tensor.transpose(MSG[b][:, s * D:(s + 1) * D], rows[:, b, s, :], ident[:, :])
                last.then_inc(back_turned, 1)

            def load_x(steps):
                for c, b, i in steps:
                    pe.wait_ge(rows_dma[b], i * 16 + 16)
                    back(0, c, b)

            chunk_pairs(pe, load_x)
            pe.wait_ge(passes_set, 1)
            P = pe.value_load(passes[0:1, 0:1], min_val=1, max_val=MAX_PASSES)
            for l, layer in enumerate(LAYERS):
                rel = layer["kind"] == REL
                r = REL_BEFORE[l]
                if rel:
                    if layer["src"] == "x":
                        pe.wait_ge(x_kept, 2 + CHUNKS * (1 + NORM_BEFORE[l]))
                    else:
                        pe.wait_ge(y_kept, 2 + CHUNKS * KEPT_BEFORE[l])

                    def own(steps):
                        for c, b, i in steps:
                            pe.wait_ge(acc_set, c + r * CHUNKS + 1)
                            nc.tensor.matmul(LIN[b][:, :], loop_w[:, layer["lin"], :],
                                             nodes[layer["src"]][:, cols(c)], start=True, stop=True).then_inc(acc_lin, 1)
                    chunk_pairs(pe, own)
                    if layer["lin"] < 3:
                        W = mix_w
                        pe.wait_ge(part, layer["lin"] + 1)
                    else:
                        W = rel_w[:, layer["lin"] - 3, :, :]
                    with pe.Fori(0, P) as p:
                        with pe.Fori(0, TURNS) as i:
                            k = pe.snap(count(P, p, r, i))
                            for h in range(2):
                                for q in (2 * h, 2 * h + 1):
                                    pe.wait_ge(gathered[q], k * 64 + 64)
                                    pe.wait_ge(onehot_ready[q], k + 1)
                                    pe.wait_ge(evacuated[(q + 2) % 4], k + 1)
                                    for t in range(4):
                                        last = nc.tensor.matmul(SUM[q % 2][:, t * KEYS:(t + 1) * KEYS], rows_in[:, 4 * q + t, :],
                                                                onehot[:, 4 * q + t, :], start=True, stop=True)
                                    last.then_inc(summed[q], 1)
                                for q in (2 * h, 2 * h + 1):
                                    pe.wait_ge(evacuated[q], k + 1 + h)
                                pe.wait_ge(added, k * RING + HALF * h + HALF)
                                for n in range(N_RELS):
                                    last = nc.tensor.matmul(MSG[h][:, 0:HALF * WIN], W[:, n, :],
                                                            sums[:, h, n, :, :].rearrange("p t v -> p (t v)"),
                                                            start=(n == 0), stop=(n == N_RELS - 1))
                                last.then_inc(messaged[h], 1)
                else:
                    pe.wait_ge(x_kept, 2 + CHUNKS * (1 + NORM_BEFORE[l]))
                    m = MEAN_BEFORE[l]
                    with pe.Fori(0, P) as p:
                        with pe.Fori(0, TURNS) as i:
                            k = pe.snap(count(P, p, m, i))
                            for h in range(2):
                                quads = (2 * h, 2 * h + 1)
                                for q in quads:
                                    pe.wait_ge(select_ready[q], k + 1 + q % 2)
                                    pe.wait_ge(spread_out[(q + 2) % 4], k + 1)
                                    for t in range(4):
                                        last = nc.tensor.matmul(SUM[q % 2][0:WIN, t * D:(t + 1) * D], near[:, 4 * q + t, :],
                                                                same[:, 4 * q + t, :], start=True, stop=True)
                                    last.then_inc(spread_ready[q], 1)
                                for q in quads:
                                    pe.wait_ge(spread_out[q], k + 1 + h)
                                    pe.wait_ge(win_in[q], k * 64 + 64)
                                    pe.wait_ge(scat_ready[(q + 2) % 4], k + 1 + h)
                                    for t in range(4):
                                        to_edges = spread[:, q * 512 + t * D:q * 512 + (t + 1) * D]
                                        nc.tensor.matmul(MSG[q % 2][:, t * D:(t + 1) * D], to_edges, win_rows[:, 4 * q + t, :],
                                                         start=True, stop=True)
                                        last = nc.tensor.matmul(LIN[q % 2][:, t:t + 1], to_edges, ones[0:WIN, 0:1],
                                                                start=True, stop=True)
                                    last.then_inc(expanded[q], 1)

                def turn(c, b):
                    pe.wait_ge(y_ready, c + l * CHUNKS + 1)
                    pe.wait_ge(rows_ready, c + l * CHUNKS + 1)
                    for s in range(SUB):
                        last = nc.tensor.transpose(SUM[b][:, s * D:(s + 1) * D], y[:, b, s * D:(s + 1) * D], ident[:, :])
                    last.then_inc(turned, 1)

                def node_phase(steps):
                    if not rel:
                        for c, b, i in steps:
                            pe.wait_ge(shares_landed[b], i * 64 + 64 * (shares_before(m, b) + 1))
                            pe.wait_ge(diag_ready, c + m * CHUNKS + 1)
                            pe.wait_ge(rows_ready, c + l * CHUNKS + 1)
                            for s in range(SUB):
                                for a in range(SHARES):
                                    last = nc.tensor.matmul(SUM[b][:, s * D:(s + 1) * D], shares_in[:, b, a, s, 0:D],
                                                            diag[:, b, s, :], start=(a == 0), stop=(a == SHARES - 1))
                            last.then_inc(agg_turned, 1)
                        for c, b, i in steps:
                            pe.wait_ge(mean_ready, c + m * CHUNKS + 1)
                            pe.wait_ge(y_ready, c + l * CHUNKS - 1)
                            nc.tensor.matmul(LIN[b][:, :], mean_wT[:, m, 0, :], xT[:, cols(c)], start=True, stop=False)
                            nc.tensor.matmul(LIN[b][:, :], mean_wT[:, m, 1, :], mean[:, b, :],
                                             start=False, stop=True).then_inc(lin_done, 1)
                    for c, b, i in steps:
                        turn(c, b)
                    if layer["norm"] and l < len(LAYERS) - 1:
                        for c, b, i in steps:
                            pe.wait_ge(rows_ready, c + l * CHUNKS + 3)
                            back(NORM_BEFORE[l] + 1, c, b)
                chunk_pairs(pe, node_phase)

        @block.vector
        def _(dve):
            steps_done = [0]

            def link(ins):
                steps_done[0] += 1
                ins.then_inc(dve_step, 1)
                dve.wait_ge(dve_step, steps_done[0])

            dve.sem_inc(added, RING)
            dve.sem_inc(rows_ready, 2)
            for q in (1, 3):
                dve.sem_inc(select_ready[q], 1)
            flat = "p c e -> p (c e)"
            dve.wait_ge(src_in, 48)
            nc.vector.tensor_copy(src_f[:, :, :], src_i[:, :, :]).then_inc(src_cast, 1)
            dve.wait_ge(dst_in, 48)
            link(nc.vector.tensor_copy(dst_f[:, :, :], dst_i[:, :, :]))
            link(nc.vector.tensor_reduce(low[:, :], dst_f[:, :, :], AX.X, ALU.min))
            link(nc.vector.scalar_tensor_tensor(type_f[:, :, :].rearrange(flat), dst_f[:, :, :].rearrange(flat), FAR,
                                                dst_f[:, :, :].rearrange(flat), ALU.is_lt, ALU.mult))
            link(nc.vector.tensor_reduce(high[:, :], type_f[:, :, :], AX.X, ALU.max))
            link(nc.vector.tensor_tensor(high[:, :], high[:, :], low[:, :], ALU.subtract))
            link(nc.vector.tensor_reduce(span[:, :], high[:, :], AX.X, ALU.max))
            link(nc.vector.tensor_scalar(low[:, :], low[:, :], float(NP - WIN), None, ALU.min))
            for c in range(BLOCKS):
                ins = nc.vector.tensor_scalar(dst_f[:, c, :], dst_f[:, c, :], low[:, c:c + 1], None, ALU.subtract)
            link(ins)
            dve.wait_ge(type_in, 48)
            link(nc.vector.tensor_copy(type_f[:, :, :], type_i[:, :, :]))
            nc.vector.scalar_tensor_tensor(type_f[:, :, :].rearrange(flat), dst_f[:, :, :].rearrange(flat), float(N_RELS),
                                           type_f[:, :, :].rearrange(flat), ALU.mult, ALU.add).then_inc(key_set, 1)
            dve.wait_ge(turned_in, 10)
            for b in range(2):
                ins = nc.vector.tensor_copy(first_window[:, b * 4 * BLOCK:(b + 1) * 4 * BLOCK], MSG[b][0:1, 0:4 * BLOCK])
            ins.then_inc(row_read, 1)
            link(nc.vector.tensor_reduce(span_row[:, 0:1], LIN[0][0:1, 0:BLOCK], AX.X, ALU.max))
            link(nc.vector.tensor_scalar(span_i[:, :], span_row[:, 0:1], float(WIN), None, ALU.add))
            nc.vector.tensor_scalar(passes[:, :], span_i[:, :], WIN.bit_length() - 1, None,
                                    ALU.logical_shift_right).then_inc(passes_set, 1)
            dve.wait_ge(passes_set, 1)
            dve.wait_ge(row_read, 1)
            dve.wait_ge(consts_set, 9)
            dve.wait_ge(tables_set, 2)
            link(nc.vector.tensor_scalar(to_spareT[:, :], srcT[:, 0:TILES], -1.0, lane[:, 0:1], ALU.mult, ALU.add))
            P = dve.value_load(passes[0:1, 0:1], min_val=1, max_val=MAX_PASSES)

            for l, layer in enumerate(LAYERS):
                rel = layer["kind"] == REL
                r, m = REL_BEFORE[l], MEAN_BEFORE[l]
                if rel and layer["lin"] < 3:
                    n = layer["lin"]
                    dve.wait_ge(tables_set, 10)
                    dve.wait_ge(weights_in, 16 * 22)
                    for b in range(N_BASES):
                        for e in range(N_RELS):
                            by = coef[:, n, e, b:b + 1]
                            if b == 0:
                                ins = nc.vector.tensor_scalar(mix_w[:, e, :], basis[:, n, b, :], by, None, ALU.mult)
                            else:
                                ins = nc.vector.scalar_tensor_tensor(mix_w[:, e, :], basis[:, n, b, :], by, mix_w[:, e, :],
                                                                     ALU.mult, ALU.add)
                        if b < N_BASES - 1:
                            link(ins)
                    ins.then_inc(part, 1)
                link(nc.vector.tensor_copy(IOTA[:, 0:KEYS + WIN], iota[:, :]))
                ins = nc.vector.tensor_copy(window[:, :], first_window[:, :])
                if rel:
                    link(ins)
                else:
                    ins.then_inc(window_set, 1)

                def onehots(h, i, k):
                    dve.wait_ge(summed[2 * h + 1], k + 1)
                    for s in range(HALF):
                        slot = HALF * h + s
                        ins = nc.vector.tensor_scalar(onehot[:, slot, :], IOTA[:, 0:KEYS], keyT[:, bass.ds(i * RING + slot, 1)],
                                                      None, ALU.is_equal)
                        if s % 4 == 3:
                            ins.then_inc(onehot_ready[2 * h + s // 4], 1)

                def adds(h, i, k):
                    _, starts = nc.values_load_multi_w_load_instructions(
                        window[0:1, bass.ds(i * RING + HALF * h, HALF)], engines=[DVE], min_val=0, max_val=NP - WIN,
                        skip_runtime_bounds_check_because="starts are destinations, held to NP - WIN on the chip")
                    dve.wait_ge(messaged[h], k + 2)
                    for s in range(HALF):
                        dve.wait_ge(added, k * RING + (RING + HALF * h + s))
                        at = bass.ds(starts[s], WIN)
                        nc.vector.tensor_tensor(acc[:, at], MSG[h][:, s * WIN:(s + 1) * WIN], acc[:, at],
                                                ALU.add).then_inc(added, 1)

                def selections(h, i, k):
                    dve.wait_ge(spread_ready[2 * h + 1], k + 1)
                    dve.wait_ge(src_all_in[h], k * 16 + 16)
                    for s in range(HALF):
                        slot = HALF * h + s
                        at = bass.ds(i * RING + slot, 1)
                        if layer["weighted"]:
                            nc.vector.tensor_scalar(near[:, slot, :], IOTA[:, KEYS:KEYS + WIN], offT[:, at], wgtT[:, at],
                                                    ALU.is_equal, ALU.mult)
                        else:
                            nc.vector.tensor_scalar(near[:, slot, :], IOTA[:, KEYS:KEYS + WIN], offT[:, at], None, ALU.is_equal)
                        ins = nc.vector.tensor_scalar(same[:, slot, :], src_all[:, h, s * D:(s + 1) * D], srcT[:, at], None,
                                                      ALU.is_equal)
                        if s % 4 == 3:
                            ins.then_inc(select_ready[2 * h + s // 4], 1)
                    dve.wait_ge(select_ready[2 * h + 1], k + 2)
                    for s in range(HALF):
                        ins = nc.vector.tensor_tensor_reduce(out=unused[:, s, :], in0=same[:, HALF * h + s, :], in1=before[:, :],
                                                             scale=1.0, scalar=0.0, op0=ALU.mult, op1=ALU.add,
                                                             accum_out=repeats[:, h, s:s + 1])
                    ins.then_inc(place_step, 1)
                    dve.wait_ge(place_step, k * 4 + (2 * h + 1))
                    dve.wait_ge(scat_ready[2 * h + 1], k + 1)
                    nc.vector.scalar_tensor_tensor(place_f[:, h, :], repeats[:, h, :], 1.0,
                                                   to_spareT[:, bass.ds(i * RING + HALF * h, HALF)],
                                                   ALU.min, ALU.mult).then_inc(place_step, 1)
                    dve.wait_ge(place_step, k * 4 + (2 * h + 2))
                    nc.vector.tensor_tensor(place_f[:, h, :], place_f[:, h, :], srcT[:, bass.ds(i * RING + HALF * h, HALF)],
                                            ALU.add).then_inc(place_ready[h], 1)

                dve.wait_ge(tables_set, 10)
                if rel:
                    dve.wait_ge(acc_set, 2 + CHUNKS * (r + 1))
                    with dve.Fori(0, P) as p:
                        onehots(0, 0, dve.snap(count(P, p, r, 0)))
                        with dve.Fori(0, TURNS - 1) as i:
                            k = dve.snap(count(P, p, r, i))
                            onehots(1, i, k)
                            adds(0, i, k)
                            onehots(0, i + 1, k + 1)
                            adds(1, i, k)
                        k = dve.snap(count(P, p, r, TURNS - 1))
                        onehots(1, TURNS - 1, k)
                        adds(0, TURNS - 1, k)
                        adds(1, TURNS - 1, k)
                        moved = dve.snap((P * r + p) * 2)
                        nc.vector.tensor_scalar(window[:, :], window[:, :], float(WIN), float(NP - WIN),
                                                ALU.add, ALU.min).then_inc(pass_moved, 1)
                        nc.vector.tensor_scalar(IOTA[:, 0:KEYS], IOTA[:, 0:KEYS], float(KEYS), None, ALU.add)\
                          .then_inc(pass_moved, 1)
                        dve.wait_ge(pass_moved, moved + 2)
                    dve.wait_ge(added, P * ((r + 1) * TILES) + RING)
                    apart(dve)
                else:
                    with dve.Fori(0, P) as p:
                        with dve.Fori(0, TURNS) as i:
                            k = dve.snap(count(P, p, m, i))
                            for h in range(2):
                                selections(h, i, k)
                        moved = dve.snap(P * m + p)
                        dve.wait_ge(expanded[3], count(P, p, m, TURNS - 1) + 2)
                        nc.vector.tensor_scalar(window[:, :], window[:, :], float(WIN), float(NP - WIN),
                                                ALU.add, ALU.min).then_inc(window_set, 1)
                        nc.vector.tensor_scalar(IOTA[:, KEYS:KEYS + WIN], IOTA[:, KEYS:KEYS + WIN], float(WIN), None,
                                                ALU.add).then_inc(comparands_moved, 1)
                        dve.wait_ge(comparands_moved, moved + 1)
                        apart(dve)

                n = NORM_BEFORE[l]

                def degrees(c, b, i):
                    at = c * 3 + m * 3 * CHUNKS
                    dve.wait_ge(shares_landed[b], i * 64 + 64 * (shares_before(m, b) + 1))
                    nc.vector.tensor_reduce(deg[:, b, :], shares_in[:, b, :, :, D].rearrange("p a k -> p k a"),
                                            AX.X, ALU.add).then_inc(deg_step, 1)
                    dve.wait_ge(deg_step, at + 1)
                    nc.vector.tensor_scalar(deg[:, b, :], deg[:, b, :], 1.0, None, ALU.max).then_inc(deg_step, 1)
                    dve.wait_ge(deg_step, at + 2)
                    nc.vector.reciprocal(deg[:, b, :], deg[:, b, :]).then_inc(deg_step, 1)
                    dve.wait_ge(deg_step, at + 3)
                    dve.wait_ge(agg_turned, c + m * CHUNKS + 1)
                    for s in range(SUB):
                        ins = nc.vector.tensor_scalar(diag[:, b, s, :], ident[:, :], deg[:, b, s:s + 1], None, ALU.mult)
                    ins.then_inc(diag_ready, 1)

                def columns(c, b):
                    dve.wait_ge(turned, c + l * CHUNKS + 1)
                    if not layer["norm"]:
                        dve.wait_ge(y_kept, c + KEPT_BEFORE[l] * CHUNKS + 1)
                    if not rel:
                        dve.wait_ge(lin_done, c + m * CHUNKS + 1)
                        ins = nc.vector.scalar_tensor_tensor(y[:, b, :], LIN[b][:, :], bias[:, layer["bias"]:layer["bias"] + 1],
                                                             xT[:, cols(c)], ALU.add, ALU.add)
                    elif not layer["add"]:
                        ins = nc.vector.tensor_scalar(y[:, b, :], acc[:, cols(c)], 0.0, None, ALU.max)
                    else:
                        ins = nc.vector.scalar_tensor_tensor(y[:, b, :], acc[:, cols(c)], 0.0,
                                                             nodes[layer["add"][0]][:, cols(c)], ALU.max, ALU.add)
                        if len(layer["add"]) == 2:
                            ins.then_inc(part, 1)
                            dve.wait_ge(part, c + 4)
                            ins = nc.vector.tensor_tensor(y[:, b, :], y[:, b, :], nodes[layer["add"][1]][:, cols(c)], ALU.add)
                    ins.then_inc(y_ready, 1)

                def moments(c, b):
                    dve.wait_ge(turned, c + l * CHUNKS + 3)
                    for s in range(SUB):
                        ins = nc.vector.bn_stats(stats[:, b, s, :], SUM[b][:, s * D:(s + 1) * D])
                    ins.then_inc(stats_done, 1)
                    dve.wait_ge(stats_done, c + n * CHUNKS + 1)
                    apart(dve)
                    for s in range(SUB):
                        ins = nc.vector.bn_aggr(mv[:, b, s, :], stats[:, b, s, :])
                    ins.then_inc(var_ready, 1)

                def normalise(c, b, i):
                    dve.wait_ge(std_ready, c + n * CHUNKS + 1)
                    nc.vector.reciprocal(rstd[:, b, :], std[:, b, :]).then_inc(rstd_done, 1)
                    dve.wait_ge(rstd_done, c + n * CHUNKS + 1)
                    dve.wait_ge(rows_dma[b], i * 16 + 16 * dma_stages(l)[b])
                    if l < len(LAYERS) - 1:
                        dve.wait_ge(back_turned, c + (n + 1) * CHUNKS + 1)
                    else:
                        dve.wait_ge(back_turned, (n + 1) * CHUNKS + 2)
                    for s in range(SUB):
                        ins = nc.vector.tensor_scalar(rows[:, b, s, :], SUM[b][:, s * D:(s + 1) * D], mv[:, b, s, 0:1],
                                                      rstd[:, b, s:s + 1], ALU.subtract, ALU.mult)
                    ins.then_inc(rows_ready, 1)

                def node_phase(steps):
                    if not rel:
                        for c, b, i in steps:
                            degrees(c, b, i)
                    for c, b, i in steps:
                        columns(c, b)
                    if layer["norm"]:
                        for c, b, i in steps:
                            moments(c, b)
                        for c, b, i in steps:
                            normalise(c, b, i)
                chunk_pairs(dve, node_phase)


_INS = ['x', 'src', 'dst', 'edge_type_8', 'edge_weight',
        'L0_gnn_coef1', 'L0_gnn_bases1', 'L0_gnn_loopw1', 'L0_gnn_bias1',
        'L0_gnn_coef2', 'L0_gnn_bases2', 'L0_gnn_loopw2', 'L0_gnn_bias2',
        'L0_gnn_coef3', 'L0_gnn_bases3', 'L0_gnn_loopw3', 'L0_gnn_bias3',
        'L1_gnn_W', 'L1_gnn_b',
        'L2_gnn_w1', 'L2_gnn_sl1', 'L2_gnn_b1', 'L2_gnn_w2', 'L2_gnn_sl2', 'L2_gnn_b2',
        'L3_gnn_W', 'L3_gnn_b']


def kernel(**inputs):
    import numpy as _np
    import concourse.bacc as _bacc
    from concourse import mybir as _mybir
    from concourse.bass_utils import run_bass_kernel_spmd as _run

    nc = _bacc.Bacc("TRN2", target_bir_lowering=False, num_devices=1)
    arrays, a = {}, {}
    for name in _INS:
        array = _np.ascontiguousarray(inputs[name])
        arrays[f"in_{name}_dram"] = array
        a[name] = nc.dram_tensor(f"in_{name}_dram", array.shape, _mybir.dt.from_np(array.dtype), kind="ExternalInput").ap()
    out = nc.dram_tensor("out_0_dram", (N_NODES, D), _mybir.dt.float32, kind="ExternalOutput").ap()
    build(nc, a['x'], a['src'], a['dst'], a['edge_type_8'], a['edge_weight'],
          [a[f'L0_gnn_coef{n}'] for n in (1, 2, 3)], [a[f'L0_gnn_bases{n}'] for n in (1, 2, 3)],
          [a['L0_gnn_loopw1'], a['L0_gnn_loopw2'], a['L0_gnn_loopw3'], a['L2_gnn_sl1'], a['L2_gnn_sl2']],
          [a['L2_gnn_w1'], a['L2_gnn_w2']], [a['L1_gnn_W'], a['L3_gnn_W']],
          [a['L0_gnn_bias1'], a['L0_gnn_bias2'], a['L0_gnn_bias3'], a['L2_gnn_b1'], a['L2_gnn_b2'],
           a['L1_gnn_b'], a['L3_gnn_b']], out)
    r = _run(nc, [arrays], core_ids=[0])
    return r.results[0]["out_0_dram"]
```

```python
import concourse.bass as bass
from concourse import mybir
from contextlib import ExitStack


F32 = mybir.dt.float32
I32 = mybir.dt.int32
ALU = mybir.AluOpType
ACT = mybir.ActivationFunctionType
AX = mybir.AxisListType
DVE = mybir.EngineType.DVE
SP = mybir.EngineType.SP

D = 128
N_NODES = 6250
N_EDGES = 106250
N_RELS = 8
N_BASES = 4
WIN = 16
KEYS = WIN * N_RELS
HALF = 8
RING = 2 * HALF
BLOCKS = 8
BLOCK = 104
TILES = BLOCKS * BLOCK
TURNS = TILES // RING
CHUNK = 512
SUB = CHUNK // D
CHUNKS = -(-N_NODES // CHUNK)
NP = CHUNKS * CHUNK
LAST = N_NODES - (CHUNKS - 1) * CHUNK
MAX_PASSES = -(-N_NODES // WIN)
FAR = 100000.0
EPS = 1e-5
SHARES = 4
SHARE_ROWS = NP + D
COLS = D + 1
CLEAR = 4
CLEAR_STEPS = SHARE_ROWS // D // CLEAR
CLEAR_LEFT = SHARE_ROWS // D - CLEAR_STEPS * CLEAR

REL, MEAN = "relational", "mean"
LAYERS = [
    dict(kind=REL, src="x", lin=0, add=("x",), norm=False),
    dict(kind=REL, src="h", lin=1, add=("h",), norm=False),
    dict(kind=REL, src="h", lin=2, add=("h", "x"), norm=True),
    dict(kind=MEAN, mean=0, weighted=True, norm=True, bias=5),
    dict(kind=REL, src="x", lin=3, add=(), norm=False),
    dict(kind=REL, src="h", lin=4, add=("x",), norm=True),
    dict(kind=MEAN, mean=1, weighted=False, norm=True, bias=6),
]
REL_BEFORE = [sum(x["kind"] == REL for x in LAYERS[:n]) for n in range(len(LAYERS) + 1)]
MEAN_BEFORE = [sum(x["kind"] == MEAN for x in LAYERS[:n]) for n in range(len(LAYERS) + 1)]
NORM_BEFORE = [sum(x["norm"] for x in LAYERS[:n]) for n in range(len(LAYERS) + 1)]
KEPT_BEFORE = [sum(not x["norm"] for x in LAYERS[:n]) for n in range(len(LAYERS) + 1)]


def chunk_loop(eng, step):
    with eng.Fori(0, CHUNKS // 4) as i:
        for j in range(4):
            step(i * 4 + j, j, i)
    for c in range(CHUNKS // 4 * 4, CHUNKS):
        step(c, c % 4, c // 4)


def chunk_pipeline(eng, step, first, start, last):
    for c in range(first, start):
        step(c, c % 4, c // 4)
    with eng.Fori(0, 2) as i:
        for k in range(start, start + 4):
            step(i * 4 + k, k % 4, i + k // 4)
    for c in range(start + 8, last):
        step(c, c % 4, c // 4)


def is_chunk(c):
    return type(c) is not int or 0 <= c < CHUNKS


def cols(c):
    return bass.ds(c * CHUNK, CHUNK)


def build(nc, x, src, dst, etype, eweight, coefs, bases, loops, rel_ws, mean_ws, biases, out):
    with ExitStack() as ctx:
        def sb(name, shape, dt=F32):
            return ctx.enter_context(nc.sbuf_tensor(name, shape, dt))

        def bank(name):
            return ctx.enter_context(nc.psum_tensor(name, [128, 512], F32))

        def sem(name):
            return ctx.enter_context(nc.semaphore(name))

        table = nc.dram_tensor("h_table", (NP, D), F32, kind="Internal").ap()
        src_pad = nc.dram_tensor("src_pad", (TILES * D,), I32, kind="Internal").ap()
        shares = [[nc.dram_tensor(f"share{m}_{a}", (SHARE_ROWS, COLS), F32, kind="Internal").ap()
                   for a in range(SHARES)] for m in range(2)]

        xT = sb("xT", [D, NP])
        hT = sb("hT", [D, NP])
        acc = sb("acc", [D, NP])
        x_rows = acc[:, :].rearrange("p (k d) -> p k d", d=D)
        nodes = {"x": xT, "h": hT}
        edges_i = sb("edges_i", [D, 3, BLOCKS * D], I32)
        src_i, dst_i, type_i = (edges_i[0:BLOCK, n, :].rearrange("p (c e) -> p c e", e=D) for n in range(3))
        low = sb("low", [BLOCK, BLOCKS])
        high = sb("high", [BLOCK, BLOCKS])
        span = sb("span", [BLOCK, 1])
        srcT = sb("srcT", [D, TILES + RING])
        offT = sb("offT", [D, TILES])
        keyT = sb("keyT", [D, TILES])
        wgtT = sb("wgtT", [D, TILES])
        to_spareT = sb("to_spareT", [D, TILES])
        first_window = sb("first_window", [1, TILES], I32)
        window = sb("window", [1, TILES], I32)
        passes = sb("passes", [1, 1], I32)
        span_row = sb("span_row", [1, 2])
        span_i = sb("span_i", [1, 1], I32)
        ident = sb("ident", [128, 128])
        ones = sb("ones", [128, 128])
        iota = sb("iota", [128, KEYS + WIN])
        eps = sb("eps", [128, 1])
        lane = sb("lane", [128, 1])
        lane_i = sb("lane_i", [128, 1], I32)
        before = sb("before", [128, 128])
        basis = sb("basis", [D, 3, N_BASES, D])
        rel_w = sb("rel_w", [D, 2, N_RELS, D])
        mix_w = sb("mix_w", [D, N_RELS, D])
        loop_w = sb("loop_w", [D, 5, D])
        mean_w = sb("mean_w", [D, 2, 2 * D])
        mean_wT = sb("mean_wT", [D, 2, 2, D])
        bias = sb("bias", [D, 7])
        coef_row = sb("coef_row", [1, 3 * N_RELS * N_BASES])
        coef = sb("coef", [128, 3, N_RELS, N_BASES])
        idx = sb("idx", [D, 2, HALF], I32)
        rows_in = sb("rows_in", [D, RING, D])
        onehot = sb("onehot", [D, RING, KEYS])
        sums = sb("sums", [D, 2, N_RELS, HALF, WIN])
        loaded = [t.rearrange("p (c e) -> p c e", e=D) for t in (
            onehot[0:BLOCK, 0:HALF, :].rearrange("p s k -> p (s k)"),
            onehot[0:BLOCK, HALF:RING, :].rearrange("p s k -> p (s k)"),
            sums[0:BLOCK, 0, :, :, :].rearrange("p r t v -> p (r t v)"),
            sums[0:BLOCK, 1, :, :, :].rearrange("p r t v -> p (r t v)"))]
        src_f, dst_f, type_f, wgt = loaded
        src_all = edges_i[:, 0:2, :]
        near = sb("near", [D, RING, WIN])
        same = onehot
        repeats = sb("repeats", [D, 2, HALF])
        place_f = sb("place_f", [D, 2, HALF])
        place = sb("place", [D, 2, HALF], I32)
        win_rows = rows_in[0:WIN, :, :]
        spread = sums[0:WIN, :, :, :, :].rearrange("p h r t v -> p (h r t v)")
        scat = sb("scat", [D, RING, COLS])
        shares_in = sb("shares_in", [D, 2, SHARES, SUB, COLS])
        deg = sb("deg", [D, 2, SUB])
        mean_rows = sb("mean_rows", [D, 2, SUB, D])
        zeros = sb("zeros", [D, CLEAR * COLS])
        y = sb("y", [D, 2, CHUNK])
        mean = sb("mean", [D, 2, CHUNK])
        unused = mean[:, :, :].rearrange("p b n -> p (b n)").rearrange("p (s d) -> p s d", d=D)
        rows = rows_in[:, :, :].rearrange("p (j k) d -> p j k d", k=SUB)
        stats = sb("stats", [128, 4, SUB, 6])
        mv = sb("mv", [128, 4, SUB, 2])
        std = sb("std", [128, 4, SUB])
        rstd = sb("rstd", [128, 4, SUB])
        shift = sb("shift", [128, 4, SUB])

        SUM = [bank("sum0"), bank("sum1")]
        MSG = [bank("msg0"), bank("msg1")]
        LIN = [bank("lin0"), bank("lin1")]
        IOTA = bank("iota_ps")
        TURNED = [*SUM, *LIN]
        AGG = bank("agg")
        MIX = IOTA

        consts_set = sem("consts_set")
        cleared = sem("cleared")
        src_in, dst_in, type_in, wgt_in = sem("src_in"), sem("dst_in"), sem("type_in"), sem("wgt_in")
        weights_in = sem("weights_in")
        dve_step = sem("dve_step")
        src_cast, off_set, key_set, low_set = sem("src_cast"), sem("off_set"), sem("key_set"), sem("low_set")
        turned_in = sem("turned_in")
        tables_set = sem("tables_set")
        wrapped = sem("wrapped")
        row_read = sem("row_read")
        passes_set = sem("passes_set")
        idx_ready = [sem(f"idx_ready{h}") for h in range(2)]
        gathered = [sem(f"gathered{s}") for s in range(RING)]
        onehot_ready = [sem(f"onehot_ready{q}") for q in range(4)]
        summed = [sem(f"summed{q}") for q in range(4)]
        evacuated = [sem(f"evacuated{q}") for q in range(4)]
        messaged = [sem(f"messaged{h}") for h in range(2)]
        added = sem("added")
        pass_moved = sem("pass_moved")
        comparands_moved = sem("comparands_moved")
        waits_passed = sem("waits_passed")
        src_padded = sem("src_padded")
        window_set = sem("window_set")
        win_in = [sem(f"win_in{q}") for q in range(4)]
        src_all_in = [sem(f"src_all_in{h}") for h in range(2)]
        select_ready = [sem(f"select_ready{q}") for q in range(4)]
        place_ready = [sem(f"place_ready{h}") for h in range(2)]
        place_step = sem("place_step")
        spread_ready = [sem(f"spread_ready{q}") for q in range(4)]
        spread_out = [sem(f"spread_out{q}") for q in range(4)]
        expanded = [sem(f"expanded{q}") for q in range(4)]
        scat_ready = [sem(f"scat_ready{q}") for q in range(4)]
        scattered = [sem(f"scattered{a}") for a in range(SHARES)]
        pass_opened = sem("pass_opened")
        all_scattered = sem("all_scattered")
        quads_left = sem("quads_left")
        shares_clear = sem("shares_clear")
        shares_landed = [sem(f"shares_landed{b}") for b in range(2)]
        shares_paired = sem("shares_paired")
        scaled, agg_turned = sem("scaled"), sem("agg_turned")
        own_ready, own_kept = sem("own_ready"), sem("own_kept")
        acc_lin, acc_set = sem("acc_lin"), sem("acc_set")
        deg_step, mean_ready, lin_done = sem("deg_step"), sem("mean_ready"), sem("lin_done")
        part = sem("part")
        residuals_added = sem("residuals_added")
        y_ready, y_kept, turned = sem("y_ready"), sem("y_kept"), sem("turned")
        stats_done, var_ready, std_ready, rstd_done = sem("stats_done"), sem("var_ready"), sem("std_ready"), sem("rstd_done")
        shift_ready = sem("shift_ready")
        rows_ready = sem("rows_ready")
        x_in = [sem(f"x_in{n}") for n in range(4)]
        rows_dma = [sem(f"rows_dma{j}") for j in range(4)]
        back_turned, x_kept = sem("back_turned"), sem("x_kept")

        block = ctx.enter_context(nc.Block())

        FULL = BLOCKS - 1
        TAIL = N_EDGES - FULL * BLOCK * D
        TAIL_ROWS, TAIL_LAST = TAIL // D, TAIL % D
        X_LOADS = ((0, 3), (3, 6), (6, 9), (9, CHUNKS))

        def dma_before(l, j):
            return l * len(range(j, CHUNKS, 4))

        def shares_before(m, b):
            return m * len(range(b, CHUNKS, 2))

        OPENED = 16
        CLEARS = 16 * 2 * SHARES * (CLEAR_STEPS + 1)
        GATHER_PASS = 16 * TURNS
        SCATTER_PASS = 16 * (RING // SHARES) * TURNS

        def count(P, p, layers_before, i):
            return P * (layers_before * TURNS) + p * TURNS + i

        def apart(eng):
            eng.sem_inc(waits_passed, 1)

        @block.sync
        def _(sp):
            for j in range(4):
                sp.sem_inc(rows_dma[j], 16)
            sp.wait_ge(cleared, 4)
            for view, tile, landed in ((src, src_i, src_in), (dst, dst_i, dst_in),
                                       (etype, type_i, type_in), (eweight, wgt, wgt_in)):
                body = FULL * BLOCK * D
                sp.dma_start(tile[:, 0:FULL, :],
                             view[0:body].rearrange("(c p e) -> p c e", p=BLOCK, e=D)).then_inc(landed, 16)
                sp.dma_start(tile[0:TAIL_ROWS, FULL, :],
                             view[body:body + TAIL_ROWS * D].rearrange("(p e) -> p e", e=D)).then_inc(landed, 16)
                sp.dma_start(tile[TAIL_ROWS:TAIL_ROWS + 1, FULL, 0:TAIL_LAST],
                             view[body + TAIL_ROWS * D:N_EDGES].rearrange("(p e) -> p e", p=1)).then_inc(landed, 16)
            for n, (c, c_end) in enumerate(X_LOADS):
                k, k_end = c * SUB, min(c_end * SUB, N_NODES // D)
                if n == len(X_LOADS) - 1:
                    sp.wait_ge(cleared, 6)
                    sp.dma_start(x_rows[0:N_NODES % D, k_end, :], x[k_end * D:N_NODES, :]).then_inc(x_in[n], 16)
                sp.dma_start(x_rows[:, k:k_end, :],
                             x[k * D:k_end * D, :].rearrange("(k p) d -> p k d", p=D)).then_inc(x_in[n], 16)
            sp.wait_ge(src_in, 48)
            sp.dma_start(src_pad.rearrange("(c p e) -> p c e", p=BLOCK, e=D), src_i).then_inc(src_padded, 16)
            sp.wait_ge(cleared, 5)
            tables = [shares[m][a].rearrange("(p r) c -> p r c", p=D) for m in range(2) for a in range(SHARES)]
            with sp.Fori(0, CLEAR_STEPS) as i:
                for n, view in enumerate(tables):
                    if n % 2 == 0:
                        sp.wait_ge(summed[3], i * 4 + (n // 2 + 2))
                        apart(sp)
                    sp.dma_start(view[:, bass.ds(i * CLEAR, CLEAR), :],
                                 zeros[:, :].rearrange("p (r c) -> p r c", c=COLS)).then_inc(shares_clear, 16)
            for view in tables:
                sp.dma_start(view[:, CLEAR_STEPS * CLEAR:, :], zeros[:, 0:CLEAR_LEFT * COLS].rearrange("p (r c) -> p r c", c=COLS))\
                  .then_inc(shares_clear, 16)
            sp.wait_ge(src_padded, 16)
            sp.wait_ge(passes_set, 1)
            P = sp.value_load(passes[0:1, 0:1], min_val=1, max_val=MAX_PASSES)
            for l, layer in enumerate(LAYERS):
                m = MEAN_BEFORE[l]
                if layer["kind"] == MEAN:
                    for j in range(4):
                        sp.wait_ge(rows_dma[j], 16 * dma_before(l, j) + 16)
                    sp.wait_ge(back_turned, 4 + CHUNKS * (1 + NORM_BEFORE[l]))
                    with sp.Fori(0, P) as p:
                        sp.wait_ge(window_set, P * m + p + (m + 1))
                        apart(sp)
                        with sp.Fori(0, TURNS) as i:
                            k = sp.snap(count(P, p, m, i))
                            for h in range(2):
                                _, starts = nc.values_load_multi_w_load_instructions(
                                    window[0:1, bass.ds(i * RING + HALF * h, HALF)], engines=[SP], min_val=0,
                                    max_val=NP - WIN,
                                    skip_runtime_bounds_check_because="starts are destinations, held to NP - WIN on the chip")
                                sp.wait_ge(select_ready[2 * h + 1], k + 1)
                                half = src_pad[bass.ds(i * (RING * D) + HALF * h * D, HALF * D)]
                                sp.dma_start(src_all[:, h, :], half.partition_broadcast(D)).then_inc(src_all_in[h], 16)
                                for s in range(HALF):
                                    q = 2 * h + s // 4
                                    if s % 4 == 0:
                                        sp.wait_ge(expanded[q], k + 1)
                                    sp.dma_start(win_rows[:, HALF * h + s, :],
                                                 table[bass.ds(starts[s], WIN), :]).then_inc(win_in[q], 16)
                    sp.wait_ge(all_scattered, m + 1)

                def load_shares(c, j):
                    sp.wait_ge(scaled, c + m * CHUNKS + 1)
                    for a in range(SHARES):
                        sp.dma_start(shares_in[:, j % 2, a, :, :],
                                     shares[m][a][cols(c), :].rearrange("(k p) d -> p k d", p=D)).then_inc(shares_landed[j % 2], 16)

                def store(c, j):
                    sp.wait_ge(rows_ready, c + l * CHUNKS + 5)
                    if l < len(LAYERS) - 1:
                        sp.dma_start(table[cols(c), :].rearrange("(k p) d -> p k d", p=D),
                                     rows[:, j, :, :]).then_inc(rows_dma[j], 16)
                    elif type(c) is int and c == CHUNKS - 1:
                        sp.dma_start(out[c * CHUNK:N_NODES, :], rows[0:LAST, j, 0, :]).then_inc(rows_dma[j], 16)
                    else:
                        sp.dma_start(out[cols(c), :].rearrange("(k p) d -> p k d", p=D),
                                     rows[:, j, :, :]).then_inc(rows_dma[j], 16)

                if layer["kind"] == REL:
                    chunk_loop(sp, lambda c, j, n: store(c, j))
                else:
                    def load_and_store(c, j, n):
                        if is_chunk(c):
                            load_shares(c, j)
                        if is_chunk(c - 5):
                            store(c - 5, (j - 5) % 4)
                    chunk_pipeline(sp, load_and_store, 0, 5, CHUNKS + 5)
            for j in range(4):
                sp.wait_ge(rows_dma[j], 16 * dma_before(len(LAYERS), j) + 16)

        @block.gpsimd
        def _(pool):
            for tile, value in ((src_i, 0), (dst_i, int(FAR)), (type_i, 0), (wgt, 0.0)):
                nc.gpsimd.memset(tile[:, FULL, :], value).then_inc(cleared, 1)
            nc.gpsimd.memset(ident[:, :], 0.0).then_inc(consts_set, 1)
            nc.gpsimd.memset(ones[:, :], 1.0).then_inc(consts_set, 1)
            nc.gpsimd.memset(eps[:, :], EPS).then_inc(consts_set, 1)
            nc.gpsimd.iota(iota[:, 0:KEYS].rearrange("p (r v) -> p r v", v=WIN), [[1, N_RELS], [N_RELS, WIN]],
                           base=0, channel_multiplier=0, allow_small_or_imprecise_dtypes=True).then_inc(consts_set, 1)
            nc.gpsimd.iota(iota[:, KEYS:KEYS + WIN], [[1, WIN]], base=0, channel_multiplier=0,
                           allow_small_or_imprecise_dtypes=True).then_inc(consts_set, 1)
            pool.wait_ge(consts_set, 5)
            nc.gpsimd.affine_select(out=ident[:, :], in_=ident[:, :], compare_op=ALU.not_equal, fill=1.0, base=0,
                                    pattern=[[-1, 128]], channel_multiplier=1).then_inc(consts_set, 1)
            nc.gpsimd.iota(lane[:, :], [[0, 1]], base=NP, channel_multiplier=1,
                           allow_small_or_imprecise_dtypes=True).then_inc(consts_set, 1)
            nc.gpsimd.iota(lane_i[:, :], [[0, 1]], base=NP, channel_multiplier=1).then_inc(consts_set, 1)
            nc.gpsimd.affine_select(out=before[:, :], in_=ones[:, :], compare_op=ALU.is_gt, fill=0.0, base=0,
                                    pattern=[[-1, 128]], channel_multiplier=1).then_inc(consts_set, 1)
            nc.gpsimd.memset(zeros[:, :], 0.0).then_inc(cleared, 1)
            nc.gpsimd.memset(acc[:, (CHUNKS - 1) * CHUNK:], 0.0).then_inc(cleared, 1)
            pool.sem_inc(quads_left, 3)
            pool.sem_inc(y_kept, 2)
            pool.wait_ge(passes_set, 1)
            P = pool.value_load(passes[0:1, 0:1], min_val=1, max_val=MAX_PASSES)
            for l, layer in enumerate(LAYERS):
                r, m = REL_BEFORE[l], MEAN_BEFORE[l]
                if layer["kind"] == MEAN:
                    opened = OPENED + SCATTER_PASS * m
                    with pool.Fori(0, P) as p:
                        with pool.Fori(0, TURNS) as i:
                            k = pool.snap(count(P, p, m, i))
                            for q in range(4):
                                for a in range(SHARES):
                                    if a == 0:
                                        pool.wait_ge(scat_ready[q], k + 2)
                                    pool.wait_ge(scattered[a], i * 64 + (opened + 16 * q))
                                    if a < SHARES - 1:
                                        apart(pool)
                                    else:
                                        pool.sem_inc(quads_left, 1)
                                    nc.gpsimd.indirect_dma_start(
                                        out=shares[m][a], out_offset=bass.IndirectOffsetOnAxis(
                                            ap=place[:, q // 2, 4 * (q % 2) + a:4 * (q % 2) + a + 1], axis=0),
                                        in_=scat[:, 4 * q + a, :], in_offset=None, compute_op=ALU.add,
                                    ).then_inc(scattered[a], 16)
                        for a in range(SHARES):
                            pool.wait_ge(scattered[a], opened + SCATTER_PASS)
                        with pool.If(p < P - 1):
                            pool.inc_swdge_sem(scattered, [SCATTER_PASS] * SHARES, mode="sub")
                    pool.sem_inc(all_scattered, 1)

                    def pair_shares(c, j, n):
                        b = j % 2
                        pool.wait_ge(shares_landed[b], n * 128 + 64 * (shares_before(m, b) + j // 2 + 1))
                        for a in (0, 2):
                            ins = nc.gpsimd.tensor_tensor(shares_in[:, b, a, :, :], shares_in[:, b, a, :, :],
                                                          shares_in[:, b, a + 1, :, :], ALU.add)
                        ins.then_inc(shares_paired, 1)
                    chunk_loop(pool, pair_shares)
                    continue
                rows_of = x if l == 0 else table
                if l:
                    for j in range(4):
                        pool.wait_ge(rows_dma[j], 16 * dma_before(l, j) + 16)
                    if LAYERS[l - 1]["norm"]:
                        pool.wait_ge(back_turned, 4 + CHUNKS * (1 + NORM_BEFORE[l]))
                with pool.Fori(0, P) as p:
                    pool.sem_inc(pass_opened, 1)
                    with pool.Fori(0, TURNS) as i:
                        k = pool.snap(count(P, p, r, i))
                        for h in range(2):
                            pool.wait_ge(idx_ready[h], k + 1)
                            pool.wait_ge(summed[2 * h + 1], k + 1)
                            apart(pool)
                            for s in range(HALF * h, HALF * (h + 1)):
                                nc.gpsimd.indirect_dma_start(
                                    out=rows_in[:, s, :], out_offset=None, in_=rows_of[:, :],
                                    in_offset=bass.IndirectOffsetOnAxis(ap=idx[:, h, s % HALF:s % HALF + 1], axis=0),
                                ).then_inc(gathered[s], 16)
                    with pool.If(p < P - 1):
                        pool.wait_ge(summed[3], count(P, p, r, TURNS) + 1)
                        apart(pool)
                        for h in range(2):
                            pool.inc_swdge_sem(gathered[HALF * h:HALF * (h + 1)], [GATHER_PASS] * HALF, mode="sub")
                if l == 1:
                    pool.wait_ge(shares_clear, CLEARS)
                    for a in range(SHARES):
                        nc.gpsimd.indirect_dma_start(
                            out=shares[0][a], out_offset=bass.IndirectOffsetOnAxis(ap=lane_i[:, 0:1], axis=0),
                            in_=zeros[:, 0:COLS], in_offset=None, compute_op=ALU.add).then_inc(scattered[a], 16)
                if not layer["norm"]:
                    def keep(c, j, n):
                        pool.wait_ge(y_ready, c + l * CHUNKS + 1)
                        nc.gpsimd.tensor_copy(hT[:, cols(c)], y[:, j % 2, :]).then_inc(y_kept, 1)
                    chunk_loop(pool, keep)
                if len(layer["add"]) == 2:
                    pool.wait_ge(acc_lin, CHUNKS * (r + 1))

                    def add_residuals(c, j, n):
                        nc.gpsimd.tensor_tensor(hT[:, cols(c)], hT[:, cols(c)], xT[:, cols(c)], ALU.add).then_inc(residuals_added, 1)
                    chunk_loop(pool, add_residuals)

        @block.scalar
        def _(act):
            act.sem_inc(evacuated[2], 1)
            act.sem_inc(evacuated[3], 1)
            for q in range(4):
                act.sem_inc(scat_ready[q], 1)
            act.sem_inc(spread_out[2], 1)
            act.sem_inc(spread_out[3], 1)
            act.sem_inc(acc_set, 2)
            act.sem_inc(x_kept, 2)
            act.wait_ge(consts_set, 3)
            act.activation(std[:, 0, 0:1], eps[:, 0:1], ACT.Sqrt)
            loads = 0
            for n in range(3):
                act.dma_start(coef_row[:, n * N_RELS * N_BASES:(n + 1) * N_RELS * N_BASES],
                              coefs[n].rearrange("(o r) b -> o (r b)", o=1)).then_inc(weights_in, 16)
                act.dma_start(basis[:, n, :, :], bases[n].rearrange("b i o -> i b o")).then_inc(weights_in, 16)
                loads += 2
            for n in range(2):
                act.dma_start(rel_w[:, n, :, :], rel_ws[n].rearrange("r i o -> i r o")).then_inc(weights_in, 16)
                act.dma_start(mean_w[:, n, :], mean_ws[n]).then_inc(weights_in, 16)
                loads += 2
            for n in range(5):
                act.dma_start(loop_w[:, n, :], loops[n]).then_inc(weights_in, 16)
                loads += 1
            for n in range(7):
                act.dma_start(bias[:, n:n + 1], biases[n].rearrange("(p o) -> p o", o=1)).then_inc(weights_in, 16)
                loads += 1
            copied = 0
            for n, (tile, banks) in enumerate(((srcT, SUM), (keyT, MSG), (offT, LIN), (wgtT, SUM))):
                for b in range(2):
                    act.wait_ge(turned_in, 2 * n + b + 1)
                    act.activation(tile[:, b * 4 * BLOCK:(b + 1) * 4 * BLOCK], banks[b][:, 0:4 * BLOCK],
                                   ACT.Copy).then_inc(tables_set, 1)
                    copied += 1
                if n == 0:
                    act.wait_ge(tables_set, 2)
                    act.activation(srcT[:, TILES:TILES + RING], srcT[:, 0:RING], ACT.Copy).then_inc(wrapped, 1)
                    for h in range(2):
                        act.activation(idx[:, h, :], srcT[:, HALF * h:HALF * (h + 1)], ACT.Copy).then_inc(idx_ready[h], 1)
                    act.wait_ge(wrapped, 1)
            act.wait_ge(turned_in, 11)
            act.activation(mean_wT[:, :, :, :].rearrange("p n s o -> p (n s o)"), MSG[0][:, :], ACT.Copy).then_inc(tables_set, 1)
            act.wait_ge(turned_in, 12)
            act.activation(coef[:, :, :, :].rearrange("p n r b -> p (n r b)"), MSG[1][:, 0:3 * N_RELS * N_BASES],
                           ACT.Copy).then_inc(tables_set, 1)
            act.wait_ge(weights_in, 16 * loads)

            def keep_x(stage, c, j):
                act.wait_ge(back_turned, c + (stage * CHUNKS + 5))
                act.activation(xT[:, cols(c)], MSG[j % 2][:, :], ACT.Copy).then_inc(x_kept, 1)

            def start_acc(layer, c, j):
                act.wait_ge(acc_lin, c + (REL_BEFORE[LAYERS.index(layer)] * CHUNKS + 1))
                act.activation(acc[:, cols(c)], LIN[j % 2][:, :], ACT.Identity,
                               bias=bias[:, layer["lin"]:layer["lin"] + 1]).then_inc(acc_set, 1)

            for c in range(CHUNKS + 1):
                if is_chunk(c):
                    keep_x(0, c, c)
                if is_chunk(c - 1):
                    start_acc(LAYERS[0], c - 1, c - 1)
            act.wait_ge(passes_set, 1)
            P = act.value_load(passes[0:1, 0:1], min_val=1, max_val=MAX_PASSES)
            for l, layer in enumerate(LAYERS):
                rel = layer["kind"] == REL
                r = REL_BEFORE[l]
                if rel:
                    if l:
                        chunk_loop(act, lambda c, j, n: start_acc(layer, c, j))
                    with act.Fori(0, P) as p:
                        with act.Fori(0, TURNS) as i:
                            k = act.snap(count(P, p, r, i))
                            for h in range(2):
                                act.wait_ge(messaged[h], k + 1)
                                for q in (2 * h, 2 * h + 1):
                                    act.wait_ge(summed[q], k + 1 + q % 2)
                                    act.activation(
                                        sums[:, h, :, 4 * (q % 2):4 * (q % 2) + 4, :].rearrange("p r t v -> p t r v"),
                                        SUM[q % 2][:, :].rearrange("p (t r v) -> p t r v", t=4, v=WIN),
                                        ACT.Copy).then_inc(evacuated[q], 1)
                                act.activation(idx[:, h, :], srcT[:, bass.ds((i + 1) * RING + h * HALF, HALF)],
                                               ACT.Copy).then_inc(idx_ready[h], 1)
                else:
                    m = MEAN_BEFORE[l]
                    with act.Fori(0, P) as p:
                        with act.Fori(0, TURNS) as i:
                            k = act.snap(count(P, p, m, i))
                            for h in range(2):
                                quads = (2 * h, 2 * h + 1)
                                for q in quads:
                                    act.wait_ge(spread_ready[q], k + 1 + q % 2)
                                    act.wait_ge(expanded[q], k + 1)
                                    act.activation(spread[:, q * 512:(q + 1) * 512], SUM[q % 2][0:WIN, :],
                                                   ACT.Copy).then_inc(spread_out[q], 1)
                                for q in quads:
                                    four = slice(4 * (q % 2), 4 * (q % 2) + 4)
                                    act.wait_ge(place_ready[h], k + 1)
                                    act.wait_ge(quads_left, k * 4 + (q + 1))
                                    act.activation(place[:, h, four], place_f[:, h, four], ACT.Copy)
                                    act.wait_ge(expanded[q], k + 2)
                                    act.activation(scat[:, 4 * q:4 * q + 4, 0:D],
                                                   MSG[q % 2][:, :].rearrange("p (t d) -> p t d", d=D), ACT.Copy)
                                    act.activation(scat[:, 4 * q:4 * q + 4, D], LIN[q % 2][:, 0:4],
                                                   ACT.Copy).then_inc(scat_ready[q], 1)
                def buffer_free(c, j, n):
                    act.wait_ge(rows_dma[j], n * 16 + (16 * dma_before(l, j) + 16))

                if not layer["norm"]:
                    def rows_out(c, j, n):
                        act.wait_ge(turned, c + (l * CHUNKS + 3))
                        buffer_free(c, j, n)
                        act.activation(rows[:, j, :, :].rearrange("p k d -> p (k d)"), TURNED[j][:, :],
                                       ACT.Copy).then_inc(rows_ready, 1)
                    chunk_loop(act, rows_out)
                    continue
                n_norm = NORM_BEFORE[l]
                last_layer = l == len(LAYERS) - 1

                def normalise(c, j, n):
                    act.wait_ge(shift_ready, c + (n_norm * CHUNKS + 1))
                    buffer_free(c, j, n)
                    if last_layer:
                        act.wait_ge(back_turned, (n_norm + 1) * CHUNKS + 4)
                    else:
                        act.wait_ge(back_turned, c + ((n_norm + 1) * CHUNKS + 1))
                    for s in range(SUB):
                        ins = act.activation(rows[:, j, s, :], TURNED[j][:, s * D:(s + 1) * D], ACT.Identity,
                                             bias=shift[:, j, s:s + 1], scale=rstd[:, j, s:s + 1])
                    ins.then_inc(rows_ready, 1)

                def deviate(c, j, n):
                    if is_chunk(c - 1):
                        normalise(c - 1, (j - 1) % 4, n if j else n - 1)
                    if is_chunk(c):
                        act.wait_ge(var_ready, c + (n_norm * CHUNKS + 1))
                        act.activation(std[:, j, :], mv[:, j, :, 1], ACT.Sqrt, bias=eps[:, 0:1]).then_inc(std_ready, 1)
                    if not rel and is_chunk(c + 3):
                        act.wait_ge(agg_turned, c + (m * CHUNKS + 4))
                        act.activation(mean[:, (j + 3) % 2, :], AGG[:, :], ACT.Copy).then_inc(mean_ready, 1)
                    if not last_layer and is_chunk(c - 2):
                        keep_x(n_norm + 1, c - 2, (j - 2) % 4)
                chunk_pipeline(act, deviate, 0 if rel else -3, 2, CHUNKS + 2)

        @block.tensor
        def _(pe):
            for q in (1, 3):
                pe.sem_inc(summed[q], 1)
            for h in range(2):
                pe.sem_inc(messaged[h], 1)
            for q in (1, 3):
                pe.sem_inc(spread_ready[q], 1)
            for q in range(4):
                pe.sem_inc(expanded[q], 1)
            pe.sem_inc(turned, 2)
            pe.sem_inc(back_turned, 4)
            pe.wait_ge(consts_set, 6)

            def turn_table(tile, banks):
                for b in range(2):
                    for c in range(4):
                        last = nc.tensor.transpose(banks[b][:, c * BLOCK:(c + 1) * BLOCK], tile[:, 4 * b + c, :],
                                                   ident[0:BLOCK, 0:BLOCK])
                    last.then_inc(turned_in, 1)

            pe.wait_ge(src_cast, 1)
            turn_table(src_f, SUM)
            pe.wait_ge(key_set, 1)
            turn_table(type_f, MSG)
            turn_table(dst_f, LIN)
            pe.wait_ge(wgt_in, 48)
            pe.wait_ge(tables_set, 2)
            turn_table(wgt, SUM)
            pe.wait_ge(tables_set, 4)
            for b in range(2):
                for c in range(4):
                    last = nc.tensor.matmul(MSG[b][0:1, c * BLOCK:(c + 1) * BLOCK], low[:, 4 * b + c:4 * b + c + 1],
                                            ident[0:BLOCK, 0:BLOCK], start=True, stop=True)
            pe.wait_ge(tables_set, 6)
            nc.tensor.matmul(LIN[0][0:1, 0:BLOCK], span[:, :], ident[0:BLOCK, 0:BLOCK],
                             start=True, stop=True).then_inc(turned_in, 2)
            pe.wait_ge(row_read, 1)
            pe.wait_ge(weights_in, 16 * 22)
            for n in range(2):
                for s in range(2):
                    last = nc.tensor.transpose(MSG[0][:, (2 * n + s) * D:(2 * n + s + 1) * D],
                                               mean_w[:, n, s * D:(s + 1) * D], ident[:, :])
            last.then_inc(turned_in, 1)
            nc.tensor.matmul(MSG[1][:, 0:3 * N_RELS * N_BASES], ones[0:1, :], coef_row[:, :],
                             start=True, stop=True).then_inc(turned_in, 1)
            pe.wait_ge(tables_set, 10)

            def back(stage, c, j, tiles):
                pe.wait_ge(x_kept, c + (stage * CHUNKS + 1))
                for s in range(SUB):
                    last = nc.tensor.transpose(MSG[j % 2][:, s * D:(s + 1) * D], tiles[:, s, :], ident[:, :])
                last.then_inc(back_turned, 1)

            def own(layer, c, j):
                r = REL_BEFORE[LAYERS.index(layer)]
                pe.wait_ge(acc_set, c + (r * CHUNKS + 1))
                nc.tensor.matmul(LIN[j % 2][:, :], loop_w[:, layer["lin"], :],
                                 nodes[layer["src"]][:, cols(c)], start=True, stop=True).then_inc(acc_lin, 1)

            pe.wait_ge(passes_set, 1)
            for c in range(CHUNKS + 1):
                for n, (c_first, _) in enumerate(X_LOADS):
                    if c == c_first:
                        pe.wait_ge(x_in[n], 32 if n == len(X_LOADS) - 1 else 16)
                if is_chunk(c):
                    back(0, c, c, x_rows[:, c * SUB:(c + 1) * SUB, :])
                if is_chunk(c - 1):
                    pe.wait_ge(x_kept, c + 2)
                    own(LAYERS[0], c - 1, c - 1)
            P = pe.value_load(passes[0:1, 0:1], min_val=1, max_val=MAX_PASSES)
            for l, layer in enumerate(LAYERS):
                rel = layer["kind"] == REL
                r = REL_BEFORE[l]
                if rel:
                    if l:
                        pe.wait_ge(rows_ready, 4 + CHUNKS * l)
                        if layer["src"] == "x":
                            pe.wait_ge(x_kept, 2 + CHUNKS * (1 + NORM_BEFORE[l]))
                        else:
                            pe.wait_ge(y_kept, 2 + CHUNKS * KEPT_BEFORE[l])
                        chunk_loop(pe, lambda c, j, n: own(layer, c, j))
                    if layer["lin"] < 3:
                        W = mix_w
                        pe.wait_ge(part, layer["lin"] + 1)
                    else:
                        W = rel_w[:, layer["lin"] - 3, :, :]
                    with pe.Fori(0, P) as p:
                        pe.wait_ge(pass_opened, P * r + p + 1)
                        apart(pe)
                        with pe.Fori(0, TURNS) as i:
                            k = pe.snap(count(P, p, r, i))
                            for h in range(2):
                                for q in (2 * h, 2 * h + 1):
                                    pe.wait_ge(onehot_ready[q], k + 1)
                                    pe.wait_ge(evacuated[(q + 2) % 4], k + 1)
                                    for t in range(4):
                                        pe.wait_ge(gathered[4 * q + t], i * 16 + (GATHER_PASS * r + 16))
                                        last = nc.tensor.matmul(SUM[q % 2][:, t * KEYS:(t + 1) * KEYS], rows_in[:, 4 * q + t, :],
                                                                onehot[:, 4 * q + t, :], start=True, stop=True)
                                    last.then_inc(summed[q], 1)
                                for q in (2 * h, 2 * h + 1):
                                    pe.wait_ge(evacuated[q], k + 1 + h)
                                pe.wait_ge(added, k * RING + HALF * h + HALF)
                                for n in range(N_RELS):
                                    last = nc.tensor.matmul(MSG[h][:, 0:HALF * WIN], W[:, n, :],
                                                            sums[:, h, n, :, :].rearrange("p t v -> p (t v)"),
                                                            start=(n == 0), stop=(n == N_RELS - 1))
                                last.then_inc(messaged[h], 1)
                else:
                    pe.wait_ge(x_kept, 2 + CHUNKS * (1 + NORM_BEFORE[l]))
                    m = MEAN_BEFORE[l]
                    with pe.Fori(0, P) as p:
                        with pe.Fori(0, TURNS) as i:
                            k = pe.snap(count(P, p, m, i))
                            for h in range(2):
                                quads = (2 * h, 2 * h + 1)
                                for q in quads:
                                    pe.wait_ge(select_ready[q], k + 1 + q % 2)
                                    pe.wait_ge(spread_out[(q + 2) % 4], k + 1)
                                    for t in range(4):
                                        last = nc.tensor.matmul(SUM[q % 2][0:WIN, t * D:(t + 1) * D], near[:, 4 * q + t, :],
                                                                same[:, 4 * q + t, :], start=True, stop=True)
                                    last.then_inc(spread_ready[q], 1)
                                for q in quads:
                                    pe.wait_ge(spread_out[q], k + 1 + h)
                                    pe.wait_ge(win_in[q], k * 64 + 64)
                                    pe.wait_ge(scat_ready[(q + 2) % 4], k + 1 + h)
                                    for t in range(4):
                                        to_edges = spread[:, q * 512 + t * D:q * 512 + (t + 1) * D]
                                        nc.tensor.matmul(MSG[q % 2][:, t * D:(t + 1) * D], to_edges, win_rows[:, 4 * q + t, :],
                                                         start=True, stop=True)
                                        last = nc.tensor.matmul(LIN[q % 2][:, t:t + 1], to_edges, ones[0:WIN, 0:1],
                                                                start=True, stop=True)
                                    last.then_inc(expanded[q], 1)

                    def own_mean(c, j, n):
                        pe.wait_ge(own_kept, c + (m * CHUNKS + 1))
                        nc.tensor.matmul(SUM[j % 2][:, :], mean_wT[:, m, 0, :], xT[:, cols(c)],
                                         start=True, stop=True).then_inc(own_ready, 1)
                    chunk_loop(pe, own_mean)

                def turn(c, j):
                    pe.wait_ge(y_ready, c + (l * CHUNKS + 1))
                    pe.wait_ge(rows_ready, c + (l * CHUNKS + 1))
                    for s in range(SUB):
                        last = nc.tensor.transpose(TURNED[j][:, s * D:(s + 1) * D], y[:, j % 2, s * D:(s + 1) * D], ident[:, :])
                    last.then_inc(turned, 1)

                def turn_mean(c, b):
                    pe.wait_ge(scaled, c + (m * CHUNKS + 3))
                    for s in range(SUB):
                        last = nc.tensor.transpose(AGG[:, s * D:(s + 1) * D], mean_rows[:, b, s, :], ident[:, :])
                    last.then_inc(agg_turned, 1)

                def mix_mean(c, b):
                    pe.wait_ge(mean_ready, c + (m * CHUNKS + 1))
                    if not (type(c) is int and c == 0):
                        pe.wait_ge(y_ready, c + l * CHUNKS)
                    nc.tensor.matmul(MIX[:, :], mean_wT[:, m, 1, :], mean[:, b, :], start=True, stop=True).then_inc(lin_done, 1)

                def node_step(c, j, n):
                    if is_chunk(c):
                        turn(c, j)
                    if not rel and is_chunk(c + 2):
                        mix_mean(c + 2, j % 2)
                    if not rel and is_chunk(c + 3):
                        turn_mean(c + 3, (j + 3) % 2)
                    if l < len(LAYERS) - 1 and is_chunk(c - 2):
                        pe.wait_ge(rows_ready, c + (l * CHUNKS + 3))
                        back(NORM_BEFORE[l] + 1, c - 2, (j - 2) % 4, rows[:, (j - 2) % 4, :, :])

                if layer["norm"]:
                    chunk_pipeline(pe, node_step, 0 if rel else -3, 2, CHUNKS + 2)
                else:
                    chunk_loop(pe, lambda c, j, n: turn(c, j))

        @block.vector
        def _(dve):
            steps_done = [0]

            def link(ins):
                steps_done[0] += 1
                ins.then_inc(dve_step, 1)
                dve.wait_ge(dve_step, steps_done[0])

            dve.sem_inc(added, RING)
            dve.sem_inc(rows_ready, 4)
            dve.sem_inc(scaled, 2)
            dve.sem_inc(own_kept, 2)
            for q in (1, 3):
                dve.sem_inc(select_ready[q], 1)
            flat = "p c e -> p (c e)"
            dve.wait_ge(src_in, 48)
            nc.vector.tensor_copy(src_f[:, :, :], src_i[:, :, :]).then_inc(src_cast, 1)
            dve.wait_ge(dst_in, 48)
            link(nc.vector.tensor_copy(dst_f[:, :, :], dst_i[:, :, :]))
            link(nc.vector.tensor_reduce(low[:, :], dst_f[:, :, :], AX.X, ALU.min))
            link(nc.vector.scalar_tensor_tensor(type_f[:, :, :].rearrange(flat), dst_f[:, :, :].rearrange(flat), FAR,
                                                dst_f[:, :, :].rearrange(flat), ALU.is_lt, ALU.mult))
            link(nc.vector.tensor_reduce(high[:, :], type_f[:, :, :], AX.X, ALU.max))
            link(nc.vector.tensor_tensor(high[:, :], high[:, :], low[:, :], ALU.subtract))
            link(nc.vector.tensor_reduce(span[:, :], high[:, :], AX.X, ALU.max))
            link(nc.vector.tensor_scalar(low[:, :], low[:, :], float(NP - WIN), None, ALU.min))
            for c in range(BLOCKS):
                ins = nc.vector.tensor_scalar(dst_f[:, c, :], dst_f[:, c, :], low[:, c:c + 1], None, ALU.subtract)
            link(ins)
            dve.wait_ge(type_in, 48)
            link(nc.vector.tensor_copy(type_f[:, :, :], type_i[:, :, :]))
            nc.vector.scalar_tensor_tensor(type_f[:, :, :].rearrange(flat), dst_f[:, :, :].rearrange(flat), float(N_RELS),
                                           type_f[:, :, :].rearrange(flat), ALU.mult, ALU.add).then_inc(key_set, 1)
            dve.wait_ge(turned_in, 10)
            for b in range(2):
                ins = nc.vector.tensor_copy(first_window[:, b * 4 * BLOCK:(b + 1) * 4 * BLOCK], MSG[b][0:1, 0:4 * BLOCK])
            ins.then_inc(row_read, 1)
            link(nc.vector.tensor_reduce(span_row[:, 0:1], LIN[0][0:1, 0:BLOCK], AX.X, ALU.max))
            link(nc.vector.tensor_scalar(span_i[:, :], span_row[:, 0:1], float(WIN), None, ALU.add))
            nc.vector.tensor_scalar(passes[:, :], span_i[:, :], WIN.bit_length() - 1, None,
                                    ALU.logical_shift_right).then_inc(passes_set, 1)
            dve.wait_ge(passes_set, 1)
            dve.wait_ge(row_read, 1)
            dve.wait_ge(consts_set, 9)
            dve.wait_ge(tables_set, 2)
            link(nc.vector.tensor_scalar(to_spareT[:, :], srcT[:, 0:TILES], -1.0, lane[:, 0:1], ALU.mult, ALU.add))
            P = dve.value_load(passes[0:1, 0:1], min_val=1, max_val=MAX_PASSES)

            for l, layer in enumerate(LAYERS):
                rel = layer["kind"] == REL
                r, m = REL_BEFORE[l], MEAN_BEFORE[l]
                if rel and layer["lin"] < 3:
                    n = layer["lin"]
                    dve.wait_ge(tables_set, 10)
                    dve.wait_ge(weights_in, 16 * 22)
                    for b in range(N_BASES):
                        for e in range(N_RELS):
                            by = coef[:, n, e, b:b + 1]
                            if b == 0:
                                ins = nc.vector.tensor_scalar(mix_w[:, e, :], basis[:, n, b, :], by, None, ALU.mult)
                            else:
                                ins = nc.vector.scalar_tensor_tensor(mix_w[:, e, :], basis[:, n, b, :], by, mix_w[:, e, :],
                                                                     ALU.mult, ALU.add)
                        if b < N_BASES - 1:
                            link(ins)
                    ins.then_inc(part, 1)
                link(nc.vector.tensor_copy(IOTA[:, 0:KEYS + WIN], iota[:, :]))
                ins = nc.vector.tensor_copy(window[:, :], first_window[:, :])
                if rel:
                    link(ins)
                else:
                    ins.then_inc(window_set, 1)

                def onehots(h, i, k):
                    dve.wait_ge(summed[2 * h + 1], k + 1)
                    for s in range(HALF):
                        slot = HALF * h + s
                        ins = nc.vector.tensor_scalar(onehot[:, slot, :], IOTA[:, 0:KEYS], keyT[:, bass.ds(i * RING + slot, 1)],
                                                      None, ALU.is_equal)
                        if s % 4 == 3:
                            ins.then_inc(onehot_ready[2 * h + s // 4], 1)

                def adds(h, i, k):
                    _, starts = nc.values_load_multi_w_load_instructions(
                        window[0:1, bass.ds(i * RING + HALF * h, HALF)], engines=[DVE], min_val=0, max_val=NP - WIN,
                        skip_runtime_bounds_check_because="starts are destinations, held to NP - WIN on the chip")
                    dve.wait_ge(messaged[h], k + 2)
                    for s in range(HALF):
                        dve.wait_ge(added, k * RING + (RING + HALF * h + s))
                        at = bass.ds(starts[s], WIN)
                        nc.vector.tensor_tensor(acc[:, at], MSG[h][:, s * WIN:(s + 1) * WIN], acc[:, at],
                                                ALU.add).then_inc(added, 1)

                def selections(h, i, k):
                    dve.wait_ge(spread_ready[2 * h + 1], k + 1)
                    dve.wait_ge(src_all_in[h], k * 16 + 16)
                    for s in range(HALF):
                        slot = HALF * h + s
                        at = bass.ds(i * RING + slot, 1)
                        if layer["weighted"]:
                            nc.vector.tensor_scalar(near[:, slot, :], IOTA[:, KEYS:KEYS + WIN], offT[:, at], wgtT[:, at],
                                                    ALU.is_equal, ALU.mult)
                        else:
                            nc.vector.tensor_scalar(near[:, slot, :], IOTA[:, KEYS:KEYS + WIN], offT[:, at], None, ALU.is_equal)
                        ins = nc.vector.tensor_scalar(same[:, slot, :], src_all[:, h, s * D:(s + 1) * D], srcT[:, at], None,
                                                      ALU.is_equal)
                        if s % 4 == 3:
                            ins.then_inc(select_ready[2 * h + s // 4], 1)
                    dve.wait_ge(select_ready[2 * h + 1], k + 2)
                    for s in range(HALF):
                        ins = nc.vector.tensor_tensor_reduce(out=unused[:, s, :], in0=same[:, HALF * h + s, :], in1=before[:, :],
                                                             scale=1.0, scalar=0.0, op0=ALU.mult, op1=ALU.add,
                                                             accum_out=repeats[:, h, s:s + 1])
                    ins.then_inc(place_step, 1)
                    dve.wait_ge(place_step, k * 4 + (2 * h + 1))
                    dve.wait_ge(scat_ready[2 * h + 1], k + 1)
                    nc.vector.scalar_tensor_tensor(place_f[:, h, :], repeats[:, h, :], 1.0,
                                                   to_spareT[:, bass.ds(i * RING + HALF * h, HALF)],
                                                   ALU.min, ALU.mult).then_inc(place_step, 1)
                    dve.wait_ge(place_step, k * 4 + (2 * h + 2))
                    nc.vector.tensor_tensor(place_f[:, h, :], place_f[:, h, :], srcT[:, bass.ds(i * RING + HALF * h, HALF)],
                                            ALU.add).then_inc(place_ready[h], 1)

                dve.wait_ge(tables_set, 10)
                if rel:
                    dve.wait_ge(acc_set, 2 + CHUNKS * (r + 1))
                    with dve.Fori(0, P) as p:
                        onehots(0, 0, dve.snap(count(P, p, r, 0)))
                        with dve.Fori(0, TURNS - 1) as i:
                            k = dve.snap(count(P, p, r, i))
                            onehots(1, i, k)
                            adds(0, i, k)
                            onehots(0, i + 1, k + 1)
                            adds(1, i, k)
                        k = dve.snap(count(P, p, r, TURNS - 1))
                        onehots(1, TURNS - 1, k)
                        adds(0, TURNS - 1, k)
                        adds(1, TURNS - 1, k)
                        moved = dve.snap((P * r + p) * 2)
                        nc.vector.tensor_scalar(window[:, :], window[:, :], float(WIN), float(NP - WIN),
                                                ALU.add, ALU.min).then_inc(pass_moved, 1)
                        nc.vector.tensor_scalar(IOTA[:, 0:KEYS], IOTA[:, 0:KEYS], float(KEYS), None, ALU.add)\
                          .then_inc(pass_moved, 1)
                        dve.wait_ge(pass_moved, moved + 2)
                    dve.wait_ge(added, P * ((r + 1) * TILES) + RING)
                    apart(dve)
                else:
                    with dve.Fori(0, P) as p:
                        with dve.Fori(0, TURNS) as i:
                            k = dve.snap(count(P, p, m, i))
                            for h in range(2):
                                selections(h, i, k)
                        moved = dve.snap(P * m + p)
                        dve.wait_ge(expanded[3], count(P, p, m, TURNS - 1) + 2)
                        nc.vector.tensor_scalar(window[:, :], window[:, :], float(WIN), float(NP - WIN),
                                                ALU.add, ALU.min).then_inc(window_set, 1)
                        nc.vector.tensor_scalar(IOTA[:, KEYS:KEYS + WIN], IOTA[:, KEYS:KEYS + WIN], float(WIN), None,
                                                ALU.add).then_inc(comparands_moved, 1)
                        dve.wait_ge(comparands_moved, moved + 1)
                        apart(dve)

                n_norm = NORM_BEFORE[l]
                if not rel:
                    def keep_own(c, j, n):
                        dve.wait_ge(own_ready, c + (m * CHUNKS + 1))
                        nc.vector.scalar_tensor_tensor(acc[:, cols(c)], SUM[j % 2][:, :], bias[:, layer["bias"]:layer["bias"] + 1],
                                                       xT[:, cols(c)], ALU.add, ALU.add).then_inc(own_kept, 1)
                    chunk_loop(dve, keep_own)
                    dve.wait_ge(own_kept, (m + 1) * CHUNKS + 2)

                def means(c, b):
                    at = c * 3 + m * 3 * CHUNKS
                    dve.wait_ge(shares_paired, c + (m * CHUNKS + 1))
                    both = shares_in[:, b, 0, :, :]
                    nc.vector.tensor_tensor(both, both, shares_in[:, b, 2, :, :], ALU.add).then_inc(deg_step, 1)
                    dve.wait_ge(deg_step, at + 1)
                    nc.vector.tensor_scalar(deg[:, b, :], both[:, :, D], 1.0, None, ALU.max).then_inc(deg_step, 1)
                    dve.wait_ge(deg_step, at + 2)
                    nc.vector.reciprocal(deg[:, b, :], deg[:, b, :]).then_inc(deg_step, 1)
                    dve.wait_ge(deg_step, at + 3)
                    if not (type(c) is int and c < 2):
                        dve.wait_ge(agg_turned, c + (m * CHUNKS - 1))
                    nc.vector.tensor_tensor(mean_rows[:, b, :, :], both[:, :, 0:D],
                                            deg[:, b, :].unsqueeze(2).broadcast_to([D, SUB, D]), ALU.mult).then_inc(scaled, 1)

                def columns(c, j):
                    b = j % 2
                    dve.wait_ge(turned, c + (l * CHUNKS + 1))
                    if not layer["norm"]:
                        dve.wait_ge(y_kept, c + (KEPT_BEFORE[l] * CHUNKS + 1))
                    if not rel:
                        dve.wait_ge(lin_done, c + (m * CHUNKS + 1))
                        ins = nc.vector.tensor_tensor(y[:, b, :], MIX[:, :], acc[:, cols(c)], ALU.add)
                    elif not layer["add"]:
                        ins = nc.vector.tensor_scalar(y[:, b, :], acc[:, cols(c)], 0.0, None, ALU.max)
                    else:
                        if len(layer["add"]) == 2:
                            dve.wait_ge(residuals_added, c + 1)
                        ins = nc.vector.scalar_tensor_tensor(y[:, b, :], acc[:, cols(c)], 0.0,
                                                             nodes[layer["add"][0]][:, cols(c)], ALU.max, ALU.add)
                    ins.then_inc(y_ready, 1)

                def moments(c, j):
                    dve.wait_ge(turned, c + (l * CHUNKS + 3))
                    for s in range(SUB):
                        ins = nc.vector.bn_stats(stats[:, j, s, :], TURNED[j][:, s * D:(s + 1) * D])
                    ins.then_inc(stats_done, 1)

                def variances(c, j):
                    dve.wait_ge(stats_done, c + (n_norm * CHUNKS + 1))
                    apart(dve)
                    for s in range(SUB):
                        ins = nc.vector.bn_aggr(mv[:, j, s, :], stats[:, j, s, :])
                    ins.then_inc(var_ready, 1)

                def scale(c, j):
                    dve.wait_ge(std_ready, c + (n_norm * CHUNKS + 1))
                    nc.vector.reciprocal(rstd[:, j, :], std[:, j, :]).then_inc(rstd_done, 1)

                def shifts(c, j):
                    dve.wait_ge(rstd_done, c + (n_norm * CHUNKS + 1))
                    nc.vector.scalar_tensor_tensor(shift[:, j, :], mv[:, j, :, 0], -1.0, rstd[:, j, :],
                                                   ALU.mult, ALU.mult).then_inc(shift_ready, 1)

                def node_step(c, j, n):
                    if not rel and is_chunk(c + 3):
                        means(c + 3, (j + 3) % 2)
                    if is_chunk(c):
                        moments(c, j)
                    if is_chunk(c - 1):
                        scale(c - 1, (j - 1) % 4)
                    if is_chunk(c + 2):
                        columns(c + 2, (j + 2) % 4)
                    if is_chunk(c - 1):
                        shifts(c - 1, (j - 1) % 4)
                    if is_chunk(c):
                        variances(c, j)

                if layer["norm"]:
                    chunk_pipeline(dve, node_step, -2 if rel else -3, 2, CHUNKS + 1)
                else:
                    chunk_loop(dve, lambda c, j, n: columns(c, j))


_INS = ['x', 'src', 'dst', 'edge_type_8', 'edge_weight',
        'L0_gnn_coef1', 'L0_gnn_bases1', 'L0_gnn_loopw1', 'L0_gnn_bias1',
        'L0_gnn_coef2', 'L0_gnn_bases2', 'L0_gnn_loopw2', 'L0_gnn_bias2',
        'L0_gnn_coef3', 'L0_gnn_bases3', 'L0_gnn_loopw3', 'L0_gnn_bias3',
        'L1_gnn_W', 'L1_gnn_b',
        'L2_gnn_w1', 'L2_gnn_sl1', 'L2_gnn_b1', 'L2_gnn_w2', 'L2_gnn_sl2', 'L2_gnn_b2',
        'L3_gnn_W', 'L3_gnn_b']


def kernel(**inputs):
    import numpy as _np
    import concourse.bacc as _bacc
    from concourse import mybir as _mybir
    from concourse.bass_utils import run_bass_kernel_spmd as _run

    nc = _bacc.Bacc("TRN2", target_bir_lowering=False, num_devices=1)
    arrays, a = {}, {}
    for name in _INS:
        array = _np.ascontiguousarray(inputs[name])
        arrays[f"in_{name}_dram"] = array
        a[name] = nc.dram_tensor(f"in_{name}_dram", array.shape, _mybir.dt.from_np(array.dtype), kind="ExternalInput").ap()
    out = nc.dram_tensor("out_0_dram", (N_NODES, D), _mybir.dt.float32, kind="ExternalOutput").ap()
    build(nc, a['x'], a['src'], a['dst'], a['edge_type_8'], a['edge_weight'],
          [a[f'L0_gnn_coef{n}'] for n in (1, 2, 3)], [a[f'L0_gnn_bases{n}'] for n in (1, 2, 3)],
          [a['L0_gnn_loopw1'], a['L0_gnn_loopw2'], a['L0_gnn_loopw3'], a['L2_gnn_sl1'], a['L2_gnn_sl2']],
          [a['L2_gnn_w1'], a['L2_gnn_w2']], [a['L1_gnn_W'], a['L3_gnn_W']],
          [a['L0_gnn_bias1'], a['L0_gnn_bias2'], a['L0_gnn_bias3'], a['L2_gnn_b1'], a['L2_gnn_b2'],
           a['L1_gnn_b'], a['L3_gnn_b']], out)
    r = _run(nc, [arrays], core_ids=[0])
    return r.results[0]["out_0_dram"]
```

```python
import concourse.bass as bass
from concourse import mybir
from contextlib import ExitStack


F32 = mybir.dt.float32
BF16 = mybir.dt.bfloat16
I32 = mybir.dt.int32
ALU = mybir.AluOpType
ACT = mybir.ActivationFunctionType
AX = mybir.AxisListType
DVE = mybir.EngineType.DVE
SP = mybir.EngineType.SP

D = 128
N_NODES = 6250
N_EDGES = 106250
N_RELS = 8
N_BASES = 4
WIN = 16
KEYS = WIN * N_RELS
HALF = 8
RING = 2 * HALF
BLOCKS = 8
BLOCK = 104
TILES = BLOCKS * BLOCK
TURNS = TILES // RING
CHUNK = 512
SUB = CHUNK // D
CHUNKS = -(-N_NODES // CHUNK)
NP = CHUNKS * CHUNK
LAST = N_NODES - (CHUNKS - 1) * CHUNK
LAG = 4
PARTS = 3
MAX_PASSES = -(-N_NODES // WIN)
FAR = 100000.0
EPS = 1e-5
SHARES = 4
SHARE_ROWS = NP + D
COLS = D + 1
CLEAR = 4
CLEAR_STEPS = SHARE_ROWS // D // CLEAR
CLEAR_LEFT = SHARE_ROWS // D - CLEAR_STEPS * CLEAR

REL, MEAN = "relational", "mean"
LAYERS = [
    dict(kind=REL, src="x", lin=0, add=("x",), norm=False),
    dict(kind=REL, src="h", lin=1, add=("h",), norm=False),
    dict(kind=REL, src="h", lin=2, add=("h", "x"), norm=True),
    dict(kind=MEAN, weighted=True, norm=True),
    dict(kind=REL, src="x", lin=3, add=(), norm=False),
    dict(kind=REL, src="h", lin=4, add=("x",), norm=True),
    dict(kind=MEAN, weighted=False, norm=True),
]
REL_BEFORE = [sum(x["kind"] == REL for x in LAYERS[:n]) for n in range(len(LAYERS) + 1)]
MEAN_BEFORE = [sum(x["kind"] == MEAN for x in LAYERS[:n]) for n in range(len(LAYERS) + 1)]
NORM_BEFORE = [sum(x["norm"] for x in LAYERS[:n]) for n in range(len(LAYERS) + 1)]
KEPT_BEFORE = [sum(not x["norm"] for x in LAYERS[:n]) for n in range(len(LAYERS) + 1)]


def chunk_loop(eng, step):
    with eng.Fori(0, CHUNKS // 4) as i:
        for j in range(4):
            step(i * 4 + j, j, i)
    for c in range(CHUNKS // 4 * 4, CHUNKS):
        step(c, c % 4, c // 4)


def chunk_pipeline(eng, step, first, start, last, fours=2):
    for c in range(first, start):
        step(c, c % 4, c // 4)
    with eng.Fori(0, fours) as i:
        for k in range(start, start + 4):
            step(i * 4 + k, k % 4, i + k // 4)
    for c in range(start + 4 * fours, last):
        step(c, c % 4, c // 4)


def edge_passes(eng, P, more, before, turn, opened=None, moved=None):
    with eng.If(more > 0):
        with eng.Fori(0, more) as p:
            if opened:
                opened(p)
            with eng.Fori(0, TURNS) as i:
                turn(i, eng.snap(P * (before * TURNS) + p * TURNS + i))
            if moved:
                moved(p)


def edge_chunks(nc, eng, P, more, before, turn, round_end, step, last):
    def rounds(c):
        start = eng.value_load(round_end[0:1, bass.ds(c, 1)], min_val=0, max_val=TURNS)
        end = eng.value_load(round_end[0:1, bass.ds(c + 1, 1)], min_val=0, max_val=TURNS)
        with eng.If(start < end):
            with eng.Fori(0, end - start) as n:
                i = nc.s_assert_within(start + n, min_val=0, max_val=TURNS - 1,
                                       skip_runtime_bounds_check_because="rounds before end, which is TURNS at most")
                turn(i, eng.snap(P * (before * TURNS) + more * TURNS + i))
        return end

    for c in range(LAG):
        step(c, c % 2, c // 2, rounds(c))
    with eng.Fori(LAG // 2, CHUNKS // 2) as n:
        for j in range(2):
            step(n * 2 + j, j, n, rounds(n * 2 + j))
    step(CHUNKS - 1, 0, CHUNKS // 2, rounds(CHUNKS - 1))
    for c in range(CHUNKS, last):
        step(c, c % 2, c // 2, None)


def is_chunk(c):
    return type(c) is not int or 0 <= c < CHUNKS


def cols(c):
    return bass.ds(c * CHUNK, CHUNK)


def build(nc, x, x_cols, src, src_cols, dst, etype, weight_cols, coefs, bases, loops, rel_ws, mean_ws, biases, mean_biases, out):
    with ExitStack() as ctx:
        def sb(name, shape, dt=F32):
            return ctx.enter_context(nc.sbuf_tensor(name, shape, dt))

        def bank(name):
            return ctx.enter_context(nc.psum_tensor(name, [128, 512], F32))

        def sem(name):
            return ctx.enter_context(nc.semaphore(name))

        tables = [nc.dram_tensor(f"h_table{n}", (NP, D), F32, kind="Internal").ap() for n in range(2)]
        shares = [[nc.dram_tensor(f"share{m}_{a}", (SHARE_ROWS, COLS), F32, kind="Internal").ap()
                   for a in range(SHARES)] for m in range(2)]

        xT = sb("xT", [D, NP])
        hT = sb("hT", [D, NP])
        acc = sb("acc", [D, NP])
        nodes = {"x": xT, "h": hT}
        edges_i = sb("edges_i", [D, 3, BLOCKS * D], I32)
        dst_i, type_i = (edges_i[0:BLOCK, n, :].rearrange("p (c e) -> p c e", e=D) for n in range(2))
        srcT_i = edges_i[:, 2, 0:TILES + RING]
        low = sb("low", [BLOCK, BLOCKS])
        high = sb("high", [BLOCK, BLOCKS])
        span = sb("span", [BLOCK, 1])
        srcT = sb("srcT", [D, TILES + RING])
        offT = sb("offT", [D, TILES])
        keyT = sb("keyT", [D, TILES])
        wgtT = sb("wgtT", [D, TILES])
        to_spareT = sb("to_spareT", [D, TILES])
        first_window = sb("first_window", [1, TILES], I32)
        window = sb("window", [1, TILES], I32)
        passes = sb("passes", [1, 2], I32)
        round_end = sb("round_end", [1, CHUNKS + 1], I32)
        tile_i = sb("tile_i", [BLOCK, BLOCKS], I32)
        tile_round = sb("tile_round", [BLOCK, BLOCKS])
        chunk_end = sb("chunk_end", [BLOCK, CHUNKS])
        begun = sb("begun", [BLOCK, CHUNKS, BLOCKS])
        begun_last = sb("begun_last", [BLOCK, CHUNKS])
        chunk_round = sb("chunk_round", [CHUNKS, 1])
        span_row = sb("span_row", [1, 2])
        span_i = sb("span_i", [1, 2], I32)
        ident = sb("ident", [128, 128])
        ones = sb("ones", [128, 128])
        iota = sb("iota", [128, KEYS + WIN])
        eps = sb("eps", [128, 1])
        lane = sb("lane", [128, 1])
        lane_i = sb("lane_i", [128, 1], I32)
        before = sb("before", [128, 128])
        basis = sb("basis", [D, 3, N_BASES, D])
        rel_w = sb("rel_w", [D, 2, N_RELS, D])
        mix_w = sb("mix_w", [D, N_RELS, D])
        loop_w = sb("loop_w", [D, 5, D])
        mean_wT = sb("mean_wT", [D, 2, 2, D])
        bias = sb("bias", [D, 5])
        mean_bias = sb("mean_bias", [PARTS, 2 * D])
        bias_part = sb("bias_part", [PARTS, 2 * D], BF16)
        bias_part_f = sb("bias_part_f", [PARTS, PARTS, 2 * D])
        bias_parts = sb("bias_parts", [PARTS, 2 * D], BF16)
        ones_bf = sb("ones_bf", [PARTS, D], BF16)
        coef_row = sb("coef_row", [1, 3 * N_RELS * N_BASES])
        coef = sb("coef", [128, 3, N_RELS, N_BASES])
        idx = sb("idx", [D, 2, HALF], I32)
        rows_in = sb("rows_in", [D, RING, D])
        onehot = sb("onehot", [D, RING, KEYS])
        sums = sb("sums", [D, 2, N_RELS, HALF, WIN])
        dst_f, type_f = (onehot[0:BLOCK, HALF * h:HALF * (h + 1), :].rearrange("p s k -> p (s k)")
                         .rearrange("p (c e) -> p c e", e=D) for h in range(2))
        src_all = edges_i[:, 0:2, :]
        near = sb("near", [D, RING, WIN])
        same = onehot
        repeats = sb("repeats", [D, 2, HALF])
        place_f = sb("place_f", [D, 2, HALF])
        place = sb("place", [D, 2, HALF], I32)
        win_rows = rows_in[0:WIN, :, :]
        spread = sums[0:WIN, :, :, :, :].rearrange("p h r t v -> p (h r t v)")
        scat = sb("scat", [D, RING, COLS])
        shares_in = [hT[:, n * RING * COLS:(n + 1) * RING * COLS].rearrange("p (a k c) -> p a k c", a=SHARES, c=COLS)
                     for n in range(3)] + [scat[:, :, :].rearrange("p (a k) c -> p a k c", a=SHARES)]
        deg = sb("deg", [D, 2, SUB])
        mean_rows = sb("mean_rows", [D, 2, SUB, D])
        zeros = sb("zeros", [D, CLEAR * COLS])
        y = sb("y", [D, 2, CHUNK])
        mean = sb("mean", [D, 2, CHUNK])
        unused = mean[:, :, :].rearrange("p b n -> p (b n)").rearrange("p (s d) -> p s d", d=D)
        rows = sb("rows", [D, 4, SUB, D])
        stats = sb("stats", [128, 4, SUB, 6])
        mv = sb("mv", [128, 4, SUB, 2])
        std = sb("std", [128, 4, SUB])
        rstd = sb("rstd", [128, 4, SUB])
        shift = sb("shift", [128, 4, SUB])

        SUM = [bank("sum0"), bank("sum1")]
        MSG = [bank("msg0"), bank("msg1")]
        LIN = [bank("lin0"), bank("lin1")]
        IOTA = bank("iota_ps")
        TURNED = {REL: LIN, MEAN: [*SUM, *LIN]}
        AGG = bank("agg")
        BACK = {REL: [AGG, AGG], MEAN: MSG}
        MEANS = [AGG, IOTA]

        consts_set = sem("consts_set")
        zeros_set = sem("zeros_set")
        src_in, dst_in, type_in, wgt_in = sem("src_in"), sem("dst_in"), sem("type_in"), sem("wgt_in")
        weights_in, late_weights_in = sem("weights_in"), sem("late_weights_in")
        dve_step = sem("dve_step")
        src_cast, key_set, low_set = sem("src_cast"), sem("key_set"), sem("low_set")
        turned_in = sem("turned_in")
        tables_set = sem("tables_set")
        row_read = sem("row_read")
        passes_set = sem("passes_set")
        idx_ready = [sem(f"idx_ready{h}") for h in range(2)]
        gathered = [sem(f"gathered{s}") for s in range(RING)]
        onehot_ready = [sem(f"onehot_ready{q}") for q in range(4)]
        summed = [sem(f"summed{q}") for q in range(4)]
        evacuated = [sem(f"evacuated{q}") for q in range(4)]
        messaged = [sem(f"messaged{h}") for h in range(2)]
        added = sem("added")
        pass_moved = sem("pass_moved")
        comparands_moved = sem("comparands_moved")
        waits_passed = sem("waits_passed")
        window_set = sem("window_set")
        win_in = [sem(f"win_in{q}") for q in range(4)]
        src_all_in = [sem(f"src_all_in{h}") for h in range(2)]
        select_ready = [sem(f"select_ready{q}") for q in range(4)]
        place_ready = [sem(f"place_ready{h}") for h in range(2)]
        place_step = sem("place_step")
        spread_ready = [sem(f"spread_ready{q}") for q in range(4)]
        spread_out = [sem(f"spread_out{q}") for q in range(4)]
        expanded = [sem(f"expanded{q}") for q in range(4)]
        scat_ready = [sem(f"scat_ready{q}") for q in range(4)]
        scattered = [sem(f"scattered{a}") for a in range(SHARES)]
        pass_opened = sem("pass_opened")
        all_scattered = sem("all_scattered")
        quads_left = sem("quads_left")
        shares_clear = sem("shares_clear")
        shares_landed = [sem(f"shares_landed{j}") for j in range(4)]
        round_ends_found, chunk_rounds_found, round_ends_in, round_ends_set = (
            sem("round_ends_found"), sem("chunk_rounds_found"), sem("round_ends_in"), sem("round_ends_set"))
        shares_paired = sem("shares_paired")
        scaled, agg_turned = sem("scaled"), sem("agg_turned")
        folded = sem("folded")
        acc_lin, acc_set = sem("acc_lin"), sem("acc_set")
        deg_step, mean_ready = sem("deg_step"), sem("mean_ready")
        part = sem("part")
        y_ready, y_kept = sem("y_ready"), sem("y_kept")
        turned = sem("turned")
        stats_done, var_ready, std_ready, rstd_done = sem("stats_done"), sem("var_ready"), sem("std_ready"), sem("rstd_done")
        shift_ready = sem("shift_ready")
        rows_ready = sem("rows_ready")
        x_in = [sem(f"x_in{n}") for n in range(4)]
        rows_dma = [sem(f"rows_dma{j}") for j in range(4)]
        back_turned, x_kept = sem("back_turned"), sem("x_kept")

        block = ctx.enter_context(nc.Block())

        X_LOADS = ((0, 3), (3, 6), (6, 9), (9, CHUNKS))

        def dma_before(l, j):
            return sum(len(range(j, CHUNKS, buffers)) for buffers in (2 if x["kind"] == REL else 4 for x in LAYERS[:l])
                       if j < buffers)

        def shares_before(m, j):
            return m * len(range(j, CHUNKS, 4))

        OPENED = 16
        CLEARS = 16 * 2 * SHARES * (CLEAR_STEPS + 1)
        GATHER_PASS = 16 * TURNS
        SCATTER_PASS = 16 * (RING // SHARES) * TURNS

        def count(P, p, layers_before, i):
            return P * (layers_before * TURNS) + p * TURNS + i

        def apart(eng):
            eng.sem_inc(waits_passed, 1)

        def store(eng, l, c, j):
            eng.wait_ge(rows_ready, c + (l * CHUNKS + 5))
            if l < len(LAYERS) - 1:
                eng.dma_start(tables[l % 2][cols(c), :].rearrange("(k p) d -> p k d", p=D),
                              rows[:, j, :, :]).then_inc(rows_dma[j], 16)
            elif type(c) is int and c == CHUNKS - 1:
                eng.dma_start(out[c * CHUNK:N_NODES, :], rows[0:LAST, j, 0, :]).then_inc(rows_dma[j], 16)
            else:
                eng.dma_start(out[cols(c), :].rearrange("(k p) d -> p k d", p=D),
                              rows[:, j, :, :]).then_inc(rows_dma[j], 16)

        @block.sync
        def _(sp):
            block_of = "(c p e) -> p c e"
            sp.dma_start(dst_i, dst.rearrange(block_of, p=BLOCK, e=D)).then_inc(dst_in, 16)
            sp.dma_start(srcT_i, src_cols).then_inc(src_in, 16)
            sp.dma_start(type_i, etype.rearrange(block_of, p=BLOCK, e=D)).then_inc(type_in, 16)
            for n, (c, c_end) in enumerate(X_LOADS):
                sp.dma_start(xT[:, c * CHUNK:c_end * CHUNK], x_cols[:, c * CHUNK:c_end * CHUNK]).then_inc(x_in[n], 16)

            def load_sources(h, tile):
                half = src[bass.ds(tile * D, HALF * D)]
                sp.dma_start(src_all[:, h, :], half.partition_broadcast(D)).then_inc(src_all_in[h], 16)

            sp.wait_ge(passes_set, 1)
            sp.wait_ge(key_set, 1)
            for h in range(2):
                load_sources(h, HALF * h)
            sp.wait_ge(zeros_set, 1)
            cleared = [shares[m][a].rearrange("(p r) c -> p r c", p=D) for m in range(2) for a in range(SHARES)]
            with sp.Fori(0, CLEAR_STEPS) as i:
                for n, view in enumerate(cleared):
                    if n % 2 == 0:
                        sp.wait_ge(summed[3], i * 4 + (n // 2 + 2))
                        apart(sp)
                    sp.dma_start(view[:, bass.ds(i * CLEAR, CLEAR), :],
                                 zeros[:, :].rearrange("p (r c) -> p r c", c=COLS)).then_inc(shares_clear, 16)
            for view in cleared:
                sp.dma_start(view[:, CLEAR_STEPS * CLEAR:, :], zeros[:, 0:CLEAR_LEFT * COLS].rearrange("p (r c) -> p r c", c=COLS))\
                  .then_inc(shares_clear, 16)
            P = sp.value_load(passes[0:1, 0:1], min_val=1, max_val=MAX_PASSES)
            for l, layer in enumerate(LAYERS):
                m = MEAN_BEFORE[l]
                if layer["kind"] == MEAN:
                    for j in range(4):
                        sp.wait_ge(rows_dma[j], 16 * dma_before(l, j) + 16)
                    with sp.Fori(0, P) as p:
                        sp.wait_ge(window_set, P * m + p + (m + 1))
                        apart(sp)
                        with sp.Fori(0, TURNS) as i:
                            k = sp.snap(count(P, p, m, i))
                            for h in range(2):
                                _, starts = nc.values_load_multi_w_load_instructions(
                                    window[0:1, bass.ds(i * RING + HALF * h, HALF)], engines=[SP], min_val=0,
                                    max_val=NP - WIN,
                                    skip_runtime_bounds_check_because="starts are destinations, held to NP - WIN on the chip")
                                for s in range(HALF):
                                    q = 2 * h + s // 4
                                    if s % 4 == 0:
                                        sp.wait_ge(expanded[q], k + 1)
                                    sp.dma_start(win_rows[:, HALF * h + s, :],
                                                 tables[(l - 1) % 2][bass.ds(starts[s], WIN), :]).then_inc(win_in[q], 16)
                                sp.wait_ge(select_ready[2 * h + 1], k + 2)
                                load_sources(h, i * RING + (RING + HALF * h))
                    sp.wait_ge(all_scattered, m + 1)

                def load_shares(c, j):
                    sp.wait_ge(scaled, c + (m * CHUNKS + 1))
                    for a in range(SHARES):
                        sp.dma_start(shares_in[j][:, a, :, :],
                                     shares[m][a][cols(c), :].rearrange("(k p) d -> p k d", p=D)).then_inc(shares_landed[j], 16)

                def mean_step(c, j, n):
                    if is_chunk(c + 7):
                        load_shares(c + 7, (j + 3) % 4)
                    if is_chunk(c - 1):
                        store(sp, l, c - 1, (j - 1) % 4)

                if layer["kind"] == MEAN:
                    chunk_pipeline(sp, mean_step, -7, 1, CHUNKS + 1, fours=1)
            for h in range(2):
                sp.wait_ge(src_all_in[h], P * (2 * TURNS * 16) + 16)
            apart(sp)
            for j in range(4):
                sp.wait_ge(rows_dma[j], 16 * dma_before(len(LAYERS), j) + 16)

        @block.gpsimd
        def _(pool):
            nc.gpsimd.memset(ident[:, :], 0.0).then_inc(consts_set, 1)
            nc.gpsimd.memset(ones[:, :], 1.0).then_inc(consts_set, 1)
            nc.gpsimd.memset(eps[:, :], EPS).then_inc(consts_set, 1)
            nc.gpsimd.iota(iota[:, 0:KEYS].rearrange("p (r v) -> p r v", v=WIN), [[1, N_RELS], [N_RELS, WIN]],
                           base=0, channel_multiplier=0, allow_small_or_imprecise_dtypes=True).then_inc(consts_set, 1)
            nc.gpsimd.iota(iota[:, KEYS:KEYS + WIN], [[1, WIN]], base=0, channel_multiplier=0,
                           allow_small_or_imprecise_dtypes=True).then_inc(consts_set, 1)
            pool.wait_ge(consts_set, 5)
            nc.gpsimd.affine_select(out=ident[:, :], in_=ident[:, :], compare_op=ALU.not_equal, fill=1.0, base=0,
                                    pattern=[[-1, 128]], channel_multiplier=1).then_inc(consts_set, 1)
            nc.gpsimd.iota(lane[:, :], [[0, 1]], base=NP, channel_multiplier=1,
                           allow_small_or_imprecise_dtypes=True).then_inc(consts_set, 1)
            nc.gpsimd.iota(lane_i[:, :], [[0, 1]], base=NP, channel_multiplier=1).then_inc(consts_set, 1)
            nc.gpsimd.affine_select(out=before[:, :], in_=ones[:, :], compare_op=ALU.is_gt, fill=0.0, base=0,
                                    pattern=[[-1, 128]], channel_multiplier=1).then_inc(consts_set, 1)
            nc.gpsimd.memset(zeros[:, :], 0.0).then_inc(zeros_set, 1)
            nc.gpsimd.iota(tile_i[:, :], [[BLOCK, BLOCKS]], base=0, channel_multiplier=1).then_inc(consts_set, 1)
            nc.gpsimd.iota(chunk_end[:, :], [[CHUNK, CHUNKS]], base=CHUNK, channel_multiplier=0,
                           allow_small_or_imprecise_dtypes=True).then_inc(consts_set, 1)
            nc.gpsimd.memset(round_end[:, 0:1], 0).then_inc(consts_set, 1)
            pool.sem_inc(quads_left, 3)
            pool.wait_ge(passes_set, 1)
            P = pool.value_load(passes[0:1, 0:1], min_val=1, max_val=MAX_PASSES)
            more = pool.value_load(passes[0:1, 1:2], min_val=0, max_val=MAX_PASSES - 1)
            for l, layer in enumerate(LAYERS):
                r, m = REL_BEFORE[l], MEAN_BEFORE[l]
                if layer["kind"] == MEAN:
                    opened = OPENED + SCATTER_PASS * m
                    with pool.Fori(0, P) as p:
                        with pool.Fori(0, TURNS) as i:
                            k = pool.snap(count(P, p, m, i))
                            for q in range(4):
                                for a in range(SHARES):
                                    if a == 0:
                                        pool.wait_ge(scat_ready[q], k + 2)
                                    pool.wait_ge(scattered[a], i * 64 + (opened + 16 * q))
                                    if a < SHARES - 1:
                                        apart(pool)
                                    else:
                                        pool.sem_inc(quads_left, 1)
                                    nc.gpsimd.indirect_dma_start(
                                        out=shares[m][a], out_offset=bass.IndirectOffsetOnAxis(
                                            ap=place[:, q // 2, 4 * (q % 2) + a:4 * (q % 2) + a + 1], axis=0),
                                        in_=scat[:, 4 * q + a, :], in_offset=None, compute_op=ALU.add,
                                    ).then_inc(scattered[a], 16)
                        for a in range(SHARES):
                            pool.wait_ge(scattered[a], opened + SCATTER_PASS)
                        with pool.If(p < more):
                            pool.inc_swdge_sem(scattered, [SCATTER_PASS] * SHARES, mode="sub")
                    pool.sem_inc(all_scattered, 1)

                    def pair_shares(c, j, n):
                        pool.wait_ge(shares_landed[j], n * 64 + 64 * (shares_before(m, j) + 1))
                        for a in (0, 2):
                            ins = nc.gpsimd.tensor_tensor(shares_in[j][:, a, :, :], shares_in[j][:, a, :, :],
                                                          shares_in[j][:, a + 1, :, :], ALU.add)
                        ins.then_inc(shares_paired, 1)
                    chunk_loop(pool, pair_shares)
                    continue
                rows_of = x if l == 0 else tables[(l - 1) % 2]
                if l:
                    for j in range(4):
                        pool.wait_ge(rows_dma[j], 16 * dma_before(l, j) + 16)
                with pool.Fori(0, P) as p:
                    pool.sem_inc(pass_opened, 1)
                    with pool.Fori(0, TURNS) as i:
                        k = pool.snap(count(P, p, r, i))
                        for h in range(2):
                            pool.wait_ge(idx_ready[h], k + 1)
                            pool.wait_ge(summed[2 * h + 1], k + 1)
                            apart(pool)
                            for s in range(HALF * h, HALF * (h + 1)):
                                nc.gpsimd.indirect_dma_start(
                                    out=rows_in[:, s, :], out_offset=None, in_=rows_of[:, :],
                                    in_offset=bass.IndirectOffsetOnAxis(ap=idx[:, h, s % HALF:s % HALF + 1], axis=0),
                                ).then_inc(gathered[s], 16)
                    with pool.If(p < more):
                        pool.wait_ge(summed[3], count(P, p, r, TURNS) + 1)
                        apart(pool)
                        for h in range(2):
                            pool.inc_swdge_sem(gathered[HALF * h:HALF * (h + 1)], [GATHER_PASS] * HALF, mode="sub")
                if l == 1:
                    pool.wait_ge(shares_clear, CLEARS)
                    for a in range(SHARES):
                        nc.gpsimd.indirect_dma_start(
                            out=shares[0][a], out_offset=bass.IndirectOffsetOnAxis(ap=lane_i[:, 0:1], axis=0),
                            in_=zeros[:, 0:COLS], in_offset=None, compute_op=ALU.add).then_inc(scattered[a], 16)
        @block.scalar
        def _(act):
            act.sem_inc(evacuated[2], 1)
            act.sem_inc(evacuated[3], 1)
            for q in range(4):
                act.sem_inc(scat_ready[q], 1)
            act.sem_inc(spread_out[2], 1)
            act.sem_inc(spread_out[3], 1)
            act.sem_inc(acc_set, 2)
            act.sem_inc(x_kept, 2)
            for j in range(4):
                act.sem_inc(rows_dma[j], 16)
            act.wait_ge(consts_set, 3)
            act.activation(std[:, 0, 0:1], eps[:, 0:1], ACT.Sqrt)
            act.dma_start(loop_w[:, :, :], loops).then_inc(weights_in, 16)
            act.dma_start(bias[:, :], biases).then_inc(weights_in, 16)
            act.dma_start(coef_row[:, :], coefs).then_inc(weights_in, 16)
            act.dma_start(basis[:, :, :, :], bases).then_inc(weights_in, 16)
            act.wait_ge(src_in, 16)
            act.activation(srcT[:, :], srcT_i, ACT.Copy).then_inc(src_cast, 1)
            act.wait_ge(src_cast, 1)
            for h in range(2):
                act.activation(idx[:, h, :], srcT[:, HALF * h:HALF * (h + 1)], ACT.Copy).then_inc(idx_ready[h], 1)
            for n, (tile, banks) in enumerate(((keyT, SUM), (offT, MSG))):
                for b in range(2):
                    act.wait_ge(turned_in, 2 * n + b + 2)
                    act.activation(tile[:, b * 4 * BLOCK:(b + 1) * 4 * BLOCK], banks[b][:, 0:4 * BLOCK],
                                   ACT.Copy).then_inc(tables_set, 1)
            act.wait_ge(turned_in, 6)
            act.activation(coef[:, :, :, :].rearrange("p n r b -> p (n r b)"), AGG[:, 0:3 * N_RELS * N_BASES],
                           ACT.Copy).then_inc(tables_set, 1)
            act.wait_ge(weights_in, 16 * 4)
            act.dma_start(rel_w[:, :, :, :], rel_ws).then_inc(late_weights_in, 16)
            act.dma_start(mean_wT[:, :, :, :], mean_ws).then_inc(late_weights_in, 16)
            act.dma_start(mean_bias[:, :], mean_biases.partition_broadcast(PARTS)).then_inc(late_weights_in, 16)
            act.dma_start(wgtT[:, :], weight_cols).then_inc(wgt_in, 16)

            def keep_x(stage, c, bank):
                act.wait_ge(back_turned, c + (stage * CHUNKS + 5))
                act.activation(xT[:, cols(c)], bank[:, :], ACT.Copy).then_inc(x_kept, 1)

            def start_acc(layer, c, j):
                act.wait_ge(acc_lin, c + (REL_BEFORE[LAYERS.index(layer)] * CHUNKS + 1))
                act.activation(acc[:, cols(c)], LIN[j % 2][:, :], ACT.Identity,
                               bias=bias[:, layer["lin"]:layer["lin"] + 1]).then_inc(acc_set, 1)

            act.wait_ge(passes_set, 1)
            act.wait_ge(round_ends_set, 1)
            P = act.value_load(passes[0:1, 0:1], min_val=1, max_val=MAX_PASSES)
            more = act.value_load(passes[0:1, 1:2], min_val=0, max_val=MAX_PASSES - 1)
            for l, layer in enumerate(LAYERS):
                rel = layer["kind"] == REL
                r = REL_BEFORE[l]
                if rel:
                    chunk_loop(act, lambda c, j, n: start_acc(layer, c, j))
                    def evacuate(i, k):
                        for h in range(2):
                            act.wait_ge(messaged[h], k + 1)
                            for q in (2 * h, 2 * h + 1):
                                act.wait_ge(summed[q], k + 1 + q % 2)
                                act.activation(
                                    sums[:, h, :, 4 * (q % 2):4 * (q % 2) + 4, :].rearrange("p r t v -> p t r v"),
                                    SUM[q % 2][:, :].rearrange("p (t r v) -> p t r v", t=4, v=WIN),
                                    ACT.Copy).then_inc(evacuated[q], 1)
                            act.activation(idx[:, h, :], srcT[:, bass.ds((i + 1) * RING + h * HALF, HALF)],
                                           ACT.Copy).then_inc(idx_ready[h], 1)
                else:
                    m = MEAN_BEFORE[l]
                    with act.Fori(0, P) as p:
                        with act.Fori(0, TURNS) as i:
                            k = act.snap(count(P, p, m, i))
                            for h in range(2):
                                quads = (2 * h, 2 * h + 1)
                                for q in quads:
                                    act.wait_ge(spread_ready[q], k + 1 + q % 2)
                                    act.wait_ge(expanded[q], k + 1)
                                    act.activation(spread[:, q * 512:(q + 1) * 512], SUM[q % 2][0:WIN, :],
                                                   ACT.Copy).then_inc(spread_out[q], 1)
                                for q in quads:
                                    four = slice(4 * (q % 2), 4 * (q % 2) + 4)
                                    act.wait_ge(place_ready[h], k + 1)
                                    act.wait_ge(quads_left, k * 4 + (q + 1))
                                    act.activation(place[:, h, four], place_f[:, h, four], ACT.Copy)
                                    act.wait_ge(expanded[q], k + 2)
                                    act.activation(scat[:, 4 * q:4 * q + 4, 0:D],
                                                   MSG[q % 2][:, :].rearrange("p (t d) -> p t d", d=D), ACT.Copy)
                                    act.activation(scat[:, 4 * q:4 * q + 4, D], LIN[q % 2][:, 0:4],
                                                   ACT.Copy).then_inc(scat_ready[q], 1)
                def buffer_free(c, j, n):
                    act.wait_ge(rows_dma[j], n * 16 + (16 * dma_before(l, j) + 16))

                if not layer["norm"]:
                    def rows_out(c, j, n, end):
                        if is_chunk(c - 1):
                            act.wait_ge(turned, c + (l * CHUNKS + 2))
                            buffer_free(c - 1, 1 - j, n if j else n - 1)
                            act.activation(rows[:, 1 - j, :, :].rearrange("p k d -> p (k d)"), LIN[1 - j][:, :],
                                           ACT.Copy).then_inc(rows_ready, 1)
                        if is_chunk(c - 2):
                            store(act, l, c - 2, j)
                    edge_passes(act, P, more, r, evacuate)
                    edge_chunks(nc, act, P, more, r, evacuate, round_end, rows_out, CHUNKS + 2)
                    continue
                n_norm = NORM_BEFORE[l]
                last_layer = l == len(LAYERS) - 1

                def normalise(c, j, n):
                    act.wait_ge(shift_ready, c + (m * CHUNKS + 1))
                    buffer_free(c, j, n)
                    if last_layer:
                        act.wait_ge(back_turned, n_norm * CHUNKS + 4)
                    else:
                        act.wait_ge(back_turned, c + (n_norm * CHUNKS + 1))
                    for s in range(SUB):
                        ins = act.activation(rows[:, j, s, :], TURNED[MEAN][j][:, s * D:(s + 1) * D], ACT.Identity,
                                             bias=shift[:, j, s:s + 1], scale=rstd[:, j, s:s + 1])
                    ins.then_inc(rows_ready, 1)

                def deviate(c, j):
                    act.wait_ge(var_ready, c + (n_norm * CHUNKS + 1))
                    act.activation(std[:, j, :], mv[:, j, :, 1], ACT.Sqrt, bias=eps[:, 0:1]).then_inc(std_ready, 1)

                def rel_step(c, j, n, end):
                    if is_chunk(c - 2):
                        deviate(c - 2, j)
                    if is_chunk(c - 3):
                        store(act, l, c - 3, 1 - j)
                        keep_x(n_norm, c - 3, AGG)

                def mean_step(c, j, n):
                    if is_chunk(c + 2):
                        if not (type(c) is int and c < 0):
                            act.wait_ge(turned, c + (l * CHUNKS + 3))
                            apart(act)
                        act.activation(y[:, j % 2, :], xT[:, cols(c + 2)], ACT.Copy)
                        act.wait_ge(agg_turned, c + (m * CHUNKS + 3))
                        act.activation(mean[:, j % 2, :], MEANS[j % 2][:, :], ACT.Copy).then_inc(mean_ready, 1)
                    if is_chunk(c):
                        deviate(c, j)
                    if is_chunk(c - 1):
                        normalise(c - 1, (j - 1) % 4, n if j else n - 1)
                    if not last_layer and is_chunk(c - 2):
                        keep_x(n_norm, c - 2, MSG[j % 2])

                if rel:
                    edge_passes(act, P, more, r, evacuate)
                    edge_chunks(nc, act, P, more, r, evacuate, round_end, rel_step, CHUNKS + 3)
                else:
                    chunk_pipeline(act, mean_step, -2, 2, CHUNKS + 2)

        @block.tensor
        def _(pe):
            for q in (1, 3):
                pe.sem_inc(summed[q], 1)
            for h in range(2):
                pe.sem_inc(messaged[h], 1)
            for q in (1, 3):
                pe.sem_inc(spread_ready[q], 1)
            for q in range(4):
                pe.sem_inc(expanded[q], 1)
            pe.sem_inc(turned, 2)
            pe.sem_inc(back_turned, 4)
            pe.wait_ge(consts_set, 6)

            def turn_table(tile, banks):
                for b in range(2):
                    for c in range(4):
                        last = nc.tensor.transpose(banks[b][:, c * BLOCK:(c + 1) * BLOCK], tile[:, 4 * b + c, :],
                                                   ident[0:BLOCK, 0:BLOCK])
                    last.then_inc(turned_in, 1)

            pe.wait_ge(low_set, 1)
            for b in range(2):
                for c in range(4):
                    nc.tensor.matmul(MSG[b][0:1, c * BLOCK:(c + 1) * BLOCK], low[:, 4 * b + c:4 * b + c + 1],
                                     ident[0:BLOCK, 0:BLOCK], start=True, stop=True)
            nc.tensor.matmul(LIN[0][0:1, 0:BLOCK], span[:, :], ident[0:BLOCK, 0:BLOCK],
                             start=True, stop=True).then_inc(turned_in, 1)
            pe.wait_ge(key_set, 1)
            turn_table(type_f, SUM)
            pe.wait_ge(passes_set, 1)
            turn_table(dst_f, MSG)
            pe.wait_ge(weights_in, 16 * 4)
            nc.tensor.matmul(AGG[:, 0:3 * N_RELS * N_BASES], ones[0:1, :], coef_row[:, :],
                             start=True, stop=True).then_inc(turned_in, 1)

            def back(layer, c, j):
                kind = layer["kind"]
                n = NORM_BEFORE[LAYERS.index(layer)]
                pe.wait_ge(rows_ready, c + (LAYERS.index(layer) * CHUNKS + 5))
                pe.wait_ge(x_kept, c + (n * CHUNKS + (2 if kind == REL else 1)))
                for s in range(SUB):
                    last = nc.tensor.transpose(BACK[kind][j % 2][:, s * D:(s + 1) * D], rows[:, j, s, :], ident[:, :])
                last.then_inc(back_turned, 1)

            def own(layer, c, j):
                r = REL_BEFORE[LAYERS.index(layer)]
                pe.wait_ge(acc_set, c + (r * CHUNKS + 1))
                nc.tensor.matmul(LIN[j % 2][:, :], loop_w[:, layer["lin"], :],
                                 nodes[layer["src"]][:, cols(c)], start=True, stop=True).then_inc(acc_lin, 1)

            pe.wait_ge(round_ends_found, 1)
            pe.wait_ge(tables_set, 5)
            nc.tensor.matmul(AGG[0:CHUNKS, 0:BLOCK], begun_last[:, :], ident[0:BLOCK, 0:BLOCK],
                             start=True, stop=True).then_inc(round_ends_in, 1)
            pe.wait_ge(chunk_rounds_found, 1)
            nc.tensor.matmul(AGG[0:1, 0:CHUNKS], chunk_round[:, :], ident[0:CHUNKS, 0:CHUNKS],
                             start=True, stop=True).then_inc(round_ends_in, 1)
            pe.wait_ge(round_ends_set, 1)
            P = pe.value_load(passes[0:1, 0:1], min_val=1, max_val=MAX_PASSES)
            more = pe.value_load(passes[0:1, 1:2], min_val=0, max_val=MAX_PASSES - 1)
            for l, layer in enumerate(LAYERS):
                rel = layer["kind"] == REL
                r = REL_BEFORE[l]
                if rel:
                    if l == 0:
                        for n, (first, end) in enumerate(X_LOADS):
                            pe.wait_ge(x_in[n], 16)
                            for c in range(first, end):
                                own(layer, c, c)
                        pe.wait_ge(tables_set, 5)
                    else:
                        pe.wait_ge(rows_ready, 4 + CHUNKS * l)
                        if layer["src"] == "x":
                            pe.wait_ge(x_kept, 2 + CHUNKS * NORM_BEFORE[l])
                        else:
                            pe.wait_ge(y_kept, CHUNKS * KEPT_BEFORE[l])
                        chunk_loop(pe, lambda c, j, n: own(layer, c, j))
                    if layer["lin"] < 3:
                        W = mix_w
                        pe.wait_ge(part, layer["lin"] + 1)
                    else:
                        W = rel_w[:, layer["lin"] - 3, :, :]
                    def opened(p):
                        pe.wait_ge(pass_opened, P * r + p + 1)
                        apart(pe)

                    def messages(i, k):
                        for h in range(2):
                            for q in (2 * h, 2 * h + 1):
                                pe.wait_ge(onehot_ready[q], k + 1)
                                pe.wait_ge(evacuated[(q + 2) % 4], k + 1)
                                for t in range(4):
                                    pe.wait_ge(gathered[4 * q + t], i * 16 + (GATHER_PASS * r + 16))
                                    last = nc.tensor.matmul(SUM[q % 2][:, t * KEYS:(t + 1) * KEYS], rows_in[:, 4 * q + t, :],
                                                            onehot[:, 4 * q + t, :], start=True, stop=True)
                                last.then_inc(summed[q], 1)
                            for q in (2 * h, 2 * h + 1):
                                pe.wait_ge(evacuated[q], k + 1 + h)
                            pe.wait_ge(added, k * RING + HALF * h + HALF)
                            for n in range(N_RELS):
                                last = nc.tensor.matmul(MSG[h][:, 0:HALF * WIN], W[:, n, :],
                                                        sums[:, h, n, :, :].rearrange("p t v -> p (t v)"),
                                                        start=(n == 0), stop=(n == N_RELS - 1))
                            last.then_inc(messaged[h], 1)
                else:
                    pe.wait_ge(x_kept, 2 + CHUNKS * NORM_BEFORE[l])
                    m = MEAN_BEFORE[l]
                    with pe.Fori(0, P) as p:
                        with pe.Fori(0, TURNS) as i:
                            k = pe.snap(count(P, p, m, i))
                            for h in range(2):
                                quads = (2 * h, 2 * h + 1)
                                for q in quads:
                                    pe.wait_ge(select_ready[q], k + 1 + q % 2)
                                    pe.wait_ge(spread_out[(q + 2) % 4], k + 1)
                                    for t in range(4):
                                        last = nc.tensor.matmul(SUM[q % 2][0:WIN, t * D:(t + 1) * D], near[:, 4 * q + t, :],
                                                                same[:, 4 * q + t, :], start=True, stop=True)
                                    last.then_inc(spread_ready[q], 1)
                                for q in quads:
                                    pe.wait_ge(spread_out[q], k + 1 + h)
                                    pe.wait_ge(win_in[q], k * 64 + 64)
                                    pe.wait_ge(scat_ready[(q + 2) % 4], k + 1 + h)
                                    for t in range(4):
                                        to_edges = spread[:, q * 512 + t * D:q * 512 + (t + 1) * D]
                                        nc.tensor.matmul(MSG[q % 2][:, t * D:(t + 1) * D], to_edges, win_rows[:, 4 * q + t, :],
                                                         start=True, stop=True)
                                        last = nc.tensor.matmul(LIN[q % 2][:, t:t + 1], to_edges, ones[0:WIN, 0:1],
                                                                start=True, stop=True)
                                    last.then_inc(expanded[q], 1)


                def turn(c, j):
                    pe.wait_ge(y_ready, c + (r * CHUNKS + 1))
                    pe.wait_ge(rows_ready, c + (l * CHUNKS + 3))
                    for s in range(SUB):
                        last = nc.tensor.transpose(TURNED[REL][j][:, s * D:(s + 1) * D], y[:, j, s * D:(s + 1) * D], ident[:, :])
                    last.then_inc(turned, 1)

                def turn_mean(c, b):
                    pe.wait_ge(scaled, c + (m * CHUNKS + 5))
                    if not (type(c) is int and c < 2 and m == 0):
                        pe.wait_ge(mean_ready, c + (m * CHUNKS - 1))
                        apart(pe)
                    for s in range(SUB):
                        last = nc.tensor.transpose(MEANS[b][:, s * D:(s + 1) * D], mean_rows[:, b, s, :], ident[:, :])
                    last.then_inc(agg_turned, 1)

                def mix_mean(c, j):
                    pe.wait_ge(rows_ready, c + (l * CHUNKS + 1))
                    pe.wait_ge(mean_ready, c + (m * CHUNKS + 1))
                    new_rows = TURNED[MEAN][j]
                    nc.tensor.matmul(new_rows[:, :].rearrange("p (s d) -> p s d", d=D), ones_bf[:, :],
                                     bias_parts[:, m * D:(m + 1) * D].unsqueeze(1).broadcast_to([PARTS, SUB, D]),
                                     start=True, stop=False)
                    for s in range(SUB):
                        nc.tensor.matmul(new_rows[:, s * D:(s + 1) * D], y[:, j % 2, s * D:(s + 1) * D],
                                         mean_wT[:, m, 0, :], start=False, stop=False)
                        last = nc.tensor.matmul(new_rows[:, s * D:(s + 1) * D], mean[:, j % 2, s * D:(s + 1) * D],
                                                mean_wT[:, m, 1, :], start=False, stop=(s == SUB - 1))
                    last.then_inc(turned, 1)

                def rel_step(c, j, n, end):
                    if is_chunk(c - 1):
                        turn(c - 1, 1 - j)
                    if layer["norm"] and is_chunk(c - 3):
                        back(layer, c - 3, 1 - j)

                def mean_step(c, j, n):
                    if is_chunk(c + 2):
                        turn_mean(c + 2, j % 2)
                    if is_chunk(c + 1):
                        mix_mean(c + 1, (j + 1) % 4)
                    if l < len(LAYERS) - 1 and is_chunk(c - 2):
                        back(layer, c - 2, (j - 2) % 4)

                if rel:
                    edge_passes(pe, P, more, r, messages, opened)
                    opened(more)
                    edge_chunks(nc, pe, P, more, r, messages, round_end, rel_step, CHUNKS + 3 if layer["norm"] else CHUNKS + 1)
                else:
                    pe.wait_ge(folded, 3)
                    chunk_pipeline(pe, mean_step, -2, 2, CHUNKS + 2)

        @block.vector
        def _(dve):
            steps_done = [0]

            def link(ins):
                steps_done[0] += 1
                ins.then_inc(dve_step, 1)
                dve.wait_ge(dve_step, steps_done[0])

            dve.sem_inc(added, RING)
            dve.sem_inc(rows_ready, 4)
            dve.sem_inc(scaled, 4)
            for q in (1, 3):
                dve.sem_inc(select_ready[q], 1)
            flat = "p c e -> p (c e)"
            dve.wait_ge(dst_in, 16)
            link(nc.vector.tensor_copy(dst_f[:, :, :], dst_i[:, :, :]))
            link(nc.vector.tensor_reduce(low[:, :], dst_f[:, :, :], AX.X, ALU.min))
            link(nc.vector.scalar_tensor_tensor(type_f[:, :, :].rearrange(flat), dst_f[:, :, :].rearrange(flat), FAR,
                                                dst_f[:, :, :].rearrange(flat), ALU.is_lt, ALU.mult))
            link(nc.vector.tensor_reduce(high[:, :], type_f[:, :, :], AX.X, ALU.max))
            link(nc.vector.tensor_tensor(high[:, :], high[:, :], low[:, :], ALU.subtract))
            link(nc.vector.tensor_reduce(span[:, :], high[:, :], AX.X, ALU.max))
            nc.vector.tensor_scalar(low[:, :], low[:, :], float(NP - WIN), None, ALU.min).then_inc(low_set, 1)
            dve.wait_ge(low_set, 1)
            for c in range(BLOCKS):
                ins = nc.vector.tensor_scalar(dst_f[:, c, :], dst_f[:, c, :], low[:, c:c + 1], None, ALU.subtract)
            link(ins)
            dve.wait_ge(turned_in, 1)
            link(nc.vector.tensor_reduce(span_row[:, 0:1], LIN[0][0:1, 0:BLOCK], AX.X, ALU.max))
            for n, more in enumerate((WIN, 0)):
                ins = nc.vector.tensor_scalar(span_i[:, n:n + 1], span_row[:, 0:1], float(more), None, ALU.add)
            link(ins)
            for b in range(2):
                ins = nc.vector.tensor_copy(first_window[:, b * 4 * BLOCK:(b + 1) * 4 * BLOCK], MSG[b][0:1, 0:4 * BLOCK])
            ins.then_inc(row_read, 1)
            nc.vector.tensor_scalar(passes[:, :], span_i[:, :], WIN.bit_length() - 1, None,
                                    ALU.logical_shift_right).then_inc(passes_set, 1)
            dve.wait_ge(type_in, 16)
            link(nc.vector.tensor_copy(type_f[:, :, :], type_i[:, :, :]))
            nc.vector.scalar_tensor_tensor(type_f[:, :, :].rearrange(flat), dst_f[:, :, :].rearrange(flat), float(N_RELS),
                                           type_f[:, :, :].rearrange(flat), ALU.mult, ALU.add).then_inc(key_set, 1)
            dve.wait_ge(consts_set, 12)
            link(nc.vector.tensor_scalar(tile_i[:, :], tile_i[:, :], RING.bit_length() - 1, None, ALU.logical_shift_right))
            link(nc.vector.tensor_scalar(tile_round[:, :], tile_i[:, :], 1.0, None, ALU.add))
            each = [BLOCK, CHUNKS, BLOCKS]
            link(nc.vector.tensor_tensor(begun[:, :, :], low[:, :].unsqueeze(1).broadcast_to(each),
                                         chunk_end[:, :].unsqueeze(2).broadcast_to(each), ALU.is_lt))
            link(nc.vector.tensor_tensor(begun[:, :, :], begun[:, :, :], tile_round[:, :].unsqueeze(1).broadcast_to(each),
                                         ALU.mult))
            nc.vector.tensor_reduce(begun_last[:, :], begun[:, :, :], AX.X, ALU.max).then_inc(round_ends_found, 1)
            dve.wait_ge(round_ends_in, 1)
            nc.vector.tensor_reduce(chunk_round[:, :], AGG[0:CHUNKS, 0:BLOCK], AX.X, ALU.max).then_inc(chunk_rounds_found, 1)
            dve.wait_ge(round_ends_in, 2)
            nc.vector.tensor_copy(round_end[:, 1:CHUNKS + 1], AGG[0:1, 0:CHUNKS]).then_inc(round_ends_set, 1)
            dve.wait_ge(round_ends_set, 1)
            dve.wait_ge(passes_set, 1)
            dve.wait_ge(row_read, 1)
            dve.wait_ge(consts_set, 9)
            dve.wait_ge(src_cast, 1)
            link(nc.vector.tensor_scalar(to_spareT[:, :], srcT[:, 0:TILES], -1.0, lane[:, 0:1], ALU.mult, ALU.add))
            P = dve.value_load(passes[0:1, 0:1], min_val=1, max_val=MAX_PASSES)
            more = dve.value_load(passes[0:1, 1:2], min_val=0, max_val=MAX_PASSES - 1)

            for l, layer in enumerate(LAYERS):
                rel = layer["kind"] == REL
                r, m = REL_BEFORE[l], MEAN_BEFORE[l]
                if rel and layer["lin"] < 3:
                    n = layer["lin"]
                    dve.wait_ge(tables_set, 5)
                    dve.wait_ge(weights_in, 16 * 4)
                    for b in range(N_BASES):
                        for e in range(N_RELS):
                            by = coef[:, n, e, b:b + 1]
                            if b == 0:
                                ins = nc.vector.tensor_scalar(mix_w[:, e, :], basis[:, n, b, :], by, None, ALU.mult)
                            else:
                                ins = nc.vector.scalar_tensor_tensor(mix_w[:, e, :], basis[:, n, b, :], by, mix_w[:, e, :],
                                                                     ALU.mult, ALU.add)
                        if b < N_BASES - 1:
                            link(ins)
                    ins.then_inc(part, 1)
                link(nc.vector.tensor_copy(IOTA[:, 0:KEYS + WIN], iota[:, :]))
                ins = nc.vector.tensor_copy(window[:, :], first_window[:, :])
                if rel:
                    link(ins)
                else:
                    ins.then_inc(window_set, 1)

                def onehots(h, i, k):
                    dve.wait_ge(summed[2 * h + 1], k + 1)
                    for s in range(HALF):
                        slot = HALF * h + s
                        ins = nc.vector.tensor_scalar(onehot[:, slot, :], IOTA[:, 0:KEYS], keyT[:, bass.ds(i * RING + slot, 1)],
                                                      None, ALU.is_equal)
                        if s % 4 == 3:
                            ins.then_inc(onehot_ready[2 * h + s // 4], 1)

                def adds(h, i, k):
                    _, starts = nc.values_load_multi_w_load_instructions(
                        window[0:1, bass.ds(i * RING + HALF * h, HALF)], engines=[DVE], min_val=0, max_val=NP - WIN,
                        skip_runtime_bounds_check_because="starts are destinations, held to NP - WIN on the chip")
                    dve.wait_ge(messaged[h], k + 2)
                    for s in range(HALF):
                        dve.wait_ge(added, k * RING + (RING + HALF * h + s))
                        at = bass.ds(starts[s], WIN)
                        nc.vector.tensor_tensor(acc[:, at], MSG[h][:, s * WIN:(s + 1) * WIN], acc[:, at],
                                                ALU.add).then_inc(added, 1)

                def selections(h, i, k):
                    dve.wait_ge(spread_ready[2 * h + 1], k + 1)
                    dve.wait_ge(src_all_in[h], k * 16 + 16)
                    for s in range(HALF):
                        slot = HALF * h + s
                        at = bass.ds(i * RING + slot, 1)
                        if layer["weighted"]:
                            nc.vector.tensor_scalar(near[:, slot, :], IOTA[:, KEYS:KEYS + WIN], offT[:, at], wgtT[:, at],
                                                    ALU.is_equal, ALU.mult)
                        else:
                            nc.vector.tensor_scalar(near[:, slot, :], IOTA[:, KEYS:KEYS + WIN], offT[:, at], None, ALU.is_equal)
                        ins = nc.vector.tensor_scalar(same[:, slot, :], src_all[:, h, s * D:(s + 1) * D], srcT[:, at], None,
                                                      ALU.is_equal)
                        if s % 4 == 3:
                            ins.then_inc(select_ready[2 * h + s // 4], 1)
                    dve.wait_ge(select_ready[2 * h + 1], k + 2)
                    for s in range(HALF):
                        ins = nc.vector.tensor_tensor_reduce(out=unused[:, s, :], in0=same[:, HALF * h + s, :], in1=before[:, :],
                                                             scale=1.0, scalar=0.0, op0=ALU.mult, op1=ALU.add,
                                                             accum_out=repeats[:, h, s:s + 1])
                    ins.then_inc(place_step, 1)
                    dve.wait_ge(place_step, k * 4 + (2 * h + 1))
                    dve.wait_ge(scat_ready[2 * h + 1], k + 1)
                    nc.vector.scalar_tensor_tensor(place_f[:, h, :], repeats[:, h, :], 1.0,
                                                   to_spareT[:, bass.ds(i * RING + HALF * h, HALF)],
                                                   ALU.min, ALU.mult).then_inc(place_step, 1)
                    dve.wait_ge(place_step, k * 4 + (2 * h + 2))
                    nc.vector.tensor_tensor(place_f[:, h, :], place_f[:, h, :], srcT[:, bass.ds(i * RING + HALF * h, HALF)],
                                            ALU.add).then_inc(place_ready[h], 1)

                if not rel:
                    dve.wait_ge(wgt_in, 16)
                if rel:
                    def opened(p):
                        onehots(0, 0, dve.snap(count(P, p, r, 0)))
                        dve.wait_ge(acc_set, 2 + CHUNKS * (r + 1))

                    def turn(i, k):
                        onehots(1, i, k)
                        adds(0, i, k)
                        with dve.If(i < TURNS - 1):
                            onehots(0, nc.s_assert_within(i + 1, min_val=1, max_val=TURNS - 1,
                                                          skip_runtime_bounds_check_because="the condition above"), k + 1)
                        adds(1, i, k)

                    def moved(p):
                        nc.vector.tensor_scalar(window[:, :], window[:, :], float(WIN), float(NP - WIN),
                                                ALU.add, ALU.min).then_inc(pass_moved, 1)
                        nc.vector.tensor_scalar(IOTA[:, 0:KEYS], IOTA[:, 0:KEYS], float(KEYS), None, ALU.add)\
                          .then_inc(pass_moved, 1)
                        dve.wait_ge(pass_moved, more * (2 * r) + p * 2 + 2)
                        apart(dve)
                else:
                    m = MEAN_BEFORE[l]
                    with dve.Fori(0, P) as p:
                        with dve.Fori(0, TURNS) as i:
                            k = dve.snap(count(P, p, m, i))
                            for h in range(2):
                                selections(h, i, k)
                        moved = dve.snap(P * m + p)
                        dve.wait_ge(expanded[3], count(P, p, m, TURNS - 1) + 2)
                        nc.vector.tensor_scalar(window[:, :], window[:, :], float(WIN), float(NP - WIN),
                                                ALU.add, ALU.min).then_inc(window_set, 1)
                        nc.vector.tensor_scalar(IOTA[:, KEYS:KEYS + WIN], IOTA[:, KEYS:KEYS + WIN], float(WIN), None,
                                                ALU.add).then_inc(comparands_moved, 1)
                        dve.wait_ge(comparands_moved, moved + 1)
                        apart(dve)

                    if m == 0:
                        dve.wait_ge(late_weights_in, 48)
                        for n in range(2):
                            ins = nc.vector.tensor_tensor(mean_wT[:, n, 0, :], mean_wT[:, n, 0, :], ident[:, :], ALU.add)
                        ins.then_inc(folded, 1)
                        nc.vector.tensor_copy(ones_bf[:, :], ones[0:PARTS, 0:D]).then_inc(folded, 1)
                        for n in range(PARTS):
                            link(nc.vector.tensor_copy(bias_part[:, :], mean_bias[:, :]))
                            link(nc.vector.tensor_copy(bias_part_f[:, n, :], bias_part[:, :]))
                            link(nc.vector.tensor_tensor(mean_bias[:, :], mean_bias[:, :], bias_part_f[:, n, :], ALU.subtract))
                        link(nc.vector.tensor_scalar(mean_bias[:, :], bias_part_f[:, 0, :], ident[0:PARTS, 0:1], None, ALU.mult))
                        for n in range(1, PARTS):
                            ins = nc.vector.scalar_tensor_tensor(mean_bias[:, :], bias_part_f[:, n, :], ident[0:PARTS, n:n + 1],
                                                                 mean_bias[:, :], ALU.mult, ALU.add)
                            link(ins)
                        nc.vector.tensor_copy(bias_parts[:, :], mean_bias[:, :]).then_inc(folded, 1)
                n_norm = NORM_BEFORE[l]
                def means(c, j, between):
                    b = j % 2
                    at = c * 3 + m * 3 * CHUNKS
                    dve.wait_ge(shares_paired, c + (m * CHUNKS + 1))
                    both = shares_in[j][:, 0, :, :]
                    nc.vector.tensor_tensor(both, both, shares_in[j][:, 2, :, :], ALU.add).then_inc(deg_step, 1)
                    for n in range(3):
                        between(n)
                        dve.wait_ge(deg_step, at + (n + 1))
                        if n == 0:
                            nc.vector.tensor_scalar(deg[:, b, :], both[:, :, D], 1.0, None, ALU.max).then_inc(deg_step, 1)
                        elif n == 1:
                            nc.vector.reciprocal(deg[:, b, :], deg[:, b, :]).then_inc(deg_step, 1)
                    if not (type(c) is int and c < 2):
                        dve.wait_ge(agg_turned, c + (m * CHUNKS - 1))
                    nc.vector.tensor_tensor(mean_rows[:, b, :, :], both[:, :, 0:D],
                                            deg[:, b, :].unsqueeze(2).broadcast_to([D, SUB, D]), ALU.mult).then_inc(scaled, 1)

                def columns(c, j, end):
                    dve.wait_ge(added, P * (r * TILES) + more * TILES + end * RING + RING)
                    dve.wait_ge(turned, c + (l * CHUNKS + 1))
                    if not layer["norm"] and not (type(c) is int and c < 2):
                        dve.wait_ge(y_kept, c + (KEPT_BEFORE[l] * CHUNKS - 1))
                    apart(dve)
                    if not layer["add"]:
                        ins = nc.vector.tensor_scalar(y[:, j, :], acc[:, cols(c)], 0.0, None, ALU.max)
                    else:
                        ins = nc.vector.scalar_tensor_tensor(y[:, j, :], acc[:, cols(c)], 0.0,
                                                             nodes[layer["add"][0]][:, cols(c)], ALU.max, ALU.add)
                        if len(layer["add"]) == 2:
                            ins.then_inc(part, 1)
                            dve.wait_ge(part, c + 4)
                            ins = nc.vector.tensor_tensor(y[:, j, :], y[:, j, :], nodes[layer["add"][1]][:, cols(c)], ALU.add)
                    ins.then_inc(y_ready, 1)

                def keep(c, j):
                    dve.wait_ge(y_ready, c + (r * CHUNKS + 1))
                    apart(dve)
                    nc.vector.tensor_copy(hT[:, cols(c)], y[:, j, :]).then_inc(y_kept, 1)

                def moments(c, j):
                    dve.wait_ge(turned, c + (l * CHUNKS + 3))
                    for s in range(SUB):
                        ins = nc.vector.bn_stats(stats[:, j, s, :], TURNED[layer["kind"]][j][:, s * D:(s + 1) * D])
                    ins.then_inc(stats_done, 1)

                def variances(c, j):
                    dve.wait_ge(stats_done, c + (n_norm * CHUNKS + 1))
                    apart(dve)
                    for s in range(SUB):
                        ins = nc.vector.bn_aggr(mv[:, j, s, :], stats[:, j, s, :])
                    ins.then_inc(var_ready, 1)

                def scale(c, j):
                    dve.wait_ge(std_ready, c + (n_norm * CHUNKS + 1))
                    nc.vector.reciprocal(rstd[:, j, :], std[:, j, :]).then_inc(rstd_done, 1)

                def shifts(c, j):
                    dve.wait_ge(rstd_done, c + (n_norm * CHUNKS + 1))
                    nc.vector.scalar_tensor_tensor(shift[:, j, :], mv[:, j, :, 0], -1.0, rstd[:, j, :],
                                                   ALU.mult, ALU.mult).then_inc(shift_ready, 1)

                def normalise(c, j, n):
                    dve.wait_ge(std_ready, c + (n_norm * CHUNKS + 1))
                    nc.vector.reciprocal(rstd[:, j, :], std[:, j, :]).then_inc(rstd_done, 1)
                    dve.wait_ge(rows_dma[j], n * 16 + (16 * dma_before(l, j) + 16))
                    dve.wait_ge(back_turned, c + (n_norm * CHUNKS + 3))
                    dve.wait_ge(rstd_done, c + (n_norm * CHUNKS + 1))
                    for s in range(SUB):
                        ins = nc.vector.tensor_scalar(rows[:, j, s, :], LIN[j][:, s * D:(s + 1) * D], mv[:, j, s, 0:1],
                                                      rstd[:, j, s:s + 1], ALU.subtract, ALU.mult)
                    ins.then_inc(rows_ready, 1)

                def rel_step(c, j, n, end):
                    if is_chunk(c):
                        columns(c, j, end)
                    if not layer["norm"]:
                        if is_chunk(c - 1):
                            keep(c - 1, 1 - j)
                        return
                    if is_chunk(c - 1):
                        moments(c - 1, 1 - j)
                        variances(c - 1, 1 - j)
                    if is_chunk(c - 2):
                        normalise(c - 2, j, n - 1)

                def mean_step(c, j, n):
                    def between(n):
                        if n == 0 and is_chunk(c - 1):
                            scale(c - 1, (j - 1) % 4)
                        if n == 1 and is_chunk(c - 1):
                            shifts(c - 1, (j - 1) % 4)

                    if is_chunk(c + 3):
                        means(c + 3, (j + 3) % 4, between)
                    else:
                        between(0)
                        between(1)
                    if is_chunk(c):
                        moments(c, j)
                        variances(c, j)

                if rel:
                    edge_passes(dve, P, more, r, turn, opened, moved)
                    opened(more)
                    edge_chunks(nc, dve, P, more, r, turn, round_end, rel_step, CHUNKS + 2 if layer["norm"] else CHUNKS + 1)
                else:
                    chunk_pipeline(dve, mean_step, -3, 2, CHUNKS + 1)


def kernel(x, src, dst, edge_type_8, edge_weight,
           L0_gnn_coef1, L0_gnn_bases1, L0_gnn_loopw1, L0_gnn_bias1,
           L0_gnn_coef2, L0_gnn_bases2, L0_gnn_loopw2, L0_gnn_bias2,
           L0_gnn_coef3, L0_gnn_bases3, L0_gnn_loopw3, L0_gnn_bias3,
           L1_gnn_W, L1_gnn_b,
           L2_gnn_w1, L2_gnn_sl1, L2_gnn_b1, L2_gnn_w2, L2_gnn_sl2, L2_gnn_b2,
           L3_gnn_W, L3_gnn_b):
    import numpy as _np
    import concourse.bacc as _bacc
    from concourse import mybir as _mybir
    from concourse.bass_utils import run_bass_kernel_spmd as _run

    def padded(edges, value):
        return _np.concatenate([edges, _np.full(TILES * D - N_EDGES, value, edges.dtype)])

    def by_tile(edges):
        return edges.reshape(-1, D).T

    sources = padded(_np.asarray(src), 0)
    sources = _np.concatenate([sources, sources[0:RING * D]])
    layout = {
        "x": x,
        "x_cols": _np.concatenate([_np.asarray(x).T, _np.zeros((D, NP - N_NODES), _np.float32)], axis=1),
        "src": sources,
        "src_cols": by_tile(sources),
        "dst": padded(_np.asarray(dst), int(FAR)),
        "etype": padded(_np.asarray(edge_type_8), 0),
        "weight_cols": by_tile(padded(_np.asarray(edge_weight), 0)),
        "coefs": _np.stack([L0_gnn_coef1, L0_gnn_coef2, L0_gnn_coef3]).reshape(1, -1),
        "bases": _np.stack([L0_gnn_bases1, L0_gnn_bases2, L0_gnn_bases3]).transpose(2, 0, 1, 3),
        "loops": _np.stack([L0_gnn_loopw1, L0_gnn_loopw2, L0_gnn_loopw3, L2_gnn_sl1, L2_gnn_sl2]).transpose(1, 0, 2),
        "rel_ws": _np.stack([L2_gnn_w1, L2_gnn_w2]).transpose(2, 0, 1, 3),
        "mean_ws": _np.stack([L1_gnn_W, L3_gnn_W]).reshape(2, D, 2, D).transpose(3, 0, 2, 1),
        "biases": _np.stack([L0_gnn_bias1, L0_gnn_bias2, L0_gnn_bias3, L2_gnn_b1, L2_gnn_b2]).T,
        "mean_biases": _np.concatenate([L1_gnn_b, L3_gnn_b]),
    }
    nc = _bacc.Bacc("TRN2", target_bir_lowering=False, num_devices=1)
    arrays = {f"in_{name}_dram": _np.ascontiguousarray(array) for name, array in layout.items()}
    operands = [nc.dram_tensor(name, array.shape, _mybir.dt.from_np(array.dtype), kind="ExternalInput").ap()
                for name, array in arrays.items()]
    out = nc.dram_tensor("out_0_dram", (N_NODES, D), _mybir.dt.float32, kind="ExternalOutput").ap()
    build(nc, *operands, out)
    r = _run(nc, [arrays], core_ids=[0])
    return r.results[0]["out_0_dram"]
```
